# Optimizing a Trainium2 kernel written in Bass

```python
import numpy as np
import jax
import jax.numpy as jnp

def _softmax(x, axis=-1):
    return jax.nn.softmax(x, axis=axis)

def _gelu(x):
    return jax.nn.gelu(x, approximate=True)

def _silu(x):
    return jax.nn.silu(x)

def _sigmoid(x):
    return jax.nn.sigmoid(x)

def _layernorm(x, axis=-1, eps=1e-05):
    m = jnp.mean(x, axis=axis, keepdims=True)
    v = jnp.var(x, axis=axis, keepdims=True)
    return (x - m) / jnp.sqrt(v + eps)

def _scatter_add(tgt, idx, src, axis=0):
    return tgt.at[idx].add(src)

def _segment_sum(src, seg, n):
    return jax.ops.segment_sum(src, seg, n)
kernel_name = 'mk_flamingo_gated_d1_seqx_r8_880f6f'

def setup_inputs(seed: int=0):
    np.random.seed(seed)
    _w = jnp.asarray

    def _rec_inputs():
        import jax
        import jax.numpy as jnp
        _rk = jax.random.key(seed)
        x = 7.22e-05 + 1 * jax.random.normal(jax.random.fold_in(_rk, 1), (128, 64, 128), jnp.float32)
        _lenS = 64 - jax.random.randint(jax.random.fold_in(_rk, 7), (128,), 0, max(1, 64 // 4) + 1, jnp.int32)
        _lenS2 = 64 - jax.random.randint(jax.random.fold_in(_rk, 8), (128,), 0, max(1, 64 // 4) + 1, jnp.int32)
        _ctx_1024P = jax.random.normal(jax.random.fold_in(_rk, 11), (128, 16, 128), jnp.float32)
        _ctx_1024c = jax.random.dirichlet(jax.random.fold_in(_rk, 511), 0.3 * jnp.ones((16,), jnp.float32), (128, 64))
        _ctx_1024t = jnp.einsum('bsk,bkd->bsd', _ctx_1024c, _ctx_1024P)
        _ctx_1024t = _ctx_1024t * jax.lax.rsqrt(jnp.mean(jnp.square(_ctx_1024t)) + 1e-12) * 0.953939
        ctx_1024 = 4.13588e-05 + 0.999923 * (_ctx_1024t + 0.3 * jax.random.normal(jax.random.fold_in(_rk, 611), (128, 64, 128), jnp.float32))
        _validS = jnp.arange(64)[None, :] < _lenS[:, None]
        _validS2 = jnp.arange(64)[None, :] < _lenS2[:, None]
        _causal = jnp.tril(jnp.ones((64, 64), dtype=bool))
        mask_BxSxS2_bk1 = jnp.broadcast_to(_validS2[:, None, :], (128, 64, 64))
        _g = jax.random.normal(jax.random.fold_in(_rk, 9001), (2, 1), jnp.float32)
        _g = jnp.sign(_g) * jnp.maximum(jnp.abs(_g), 1.0) + (_g == 0) * 1.0
        g_xattn = _g[0]
        g_ffn = _g[1]
        return (x, ctx_1024, mask_BxSxS2_bk1, g_xattn, g_ffn)
    x, ctx_1024, mask_BxSxS2_bk1, g_xattn, g_ffn = _rec_inputs()

    def _L0_xattn_setup():
        import jax, jax.numpy as jnp
        import numpy as np
        HEADS = 16
        D_MODEL = 128
        D_HEAD = D_MODEL // HEADS

        def _split_head(x):
            B, S, _ = x.shape
            return x.reshape(B, S, HEADS, D_HEAD).transpose(0, 2, 1, 3)
        key = jax.random.key(seed)
        ks = jax.random.split(key, 12)
        B, S = (4, 256)
        scale = D_MODEL ** (-0.5)
        inp = {'q': jax.random.normal(ks[0], (B, S, D_MODEL), jnp.float32), 'k': jax.random.normal(ks[1], (B, S, D_MODEL), jnp.float32), 'v': jax.random.normal(ks[2], (B, S, D_MODEL), jnp.float32), 'mask': jnp.triu(jnp.ones((S, S), bool), k=1)[None].repeat(B, axis=0), 'wq': jax.random.normal(ks[3], (D_MODEL, D_MODEL), jnp.float32) * scale, 'bq': jnp.zeros((D_MODEL,), jnp.float32), 'wk': jax.random.normal(ks[4], (D_MODEL, D_MODEL), jnp.float32) * scale, 'bk': jnp.zeros((D_MODEL,), jnp.float32), 'wv': jax.random.normal(ks[5], (D_MODEL, D_MODEL), jnp.float32) * scale, 'bv': jnp.zeros((D_MODEL,), jnp.float32), 'wo': jax.random.normal(ks[6], (D_MODEL, D_MODEL), jnp.float32) * scale, 'bo': jnp.zeros((D_MODEL,), jnp.float32)}
        return inp
    _L0_xattn_all = _L0_xattn_setup()
    _L0_xattn_in = {k: v for k, v in _L0_xattn_all.items() if k in ('wq', 'bq', 'wk', 'bk', 'wv', 'bv', 'wo', 'bo')}
    del _L0_xattn_all

    def _L0_ffn_setup():
        import jax, jax.numpy as jnp
        import numpy as np
        D = 128
        H = 128
        E = 8
        K = 2
        I = 2 * 128
        ROUTE_SCALE = 1.0
        key = jax.random.key(seed)
        ks = jax.random.split(key, 12)
        s = lambda *sh: 1.0 / np.sqrt(sh[-1])
        return {'x': jax.random.normal(ks[0], (1, 256, D), jnp.float32), 'gate_w': jax.random.normal(ks[1], (E, D), jnp.float32) * s(E, D), 'w1': jax.random.normal(ks[2], (E, H, D), jnp.float32) * s(H, D), 'b1': jax.random.normal(ks[3], (E, H), jnp.float32) * 0.01, 'w2': jax.random.normal(ks[4], (E, D, H), jnp.float32) * s(D, H), 'b2': jax.random.normal(ks[5], (E, D), jnp.float32) * 0.01, 'w3': jax.random.normal(ks[6], (E, H, D), jnp.float32) * s(H, D), 'b3': jax.random.normal(ks[7], (E, H), jnp.float32) * 0.01, 'sw1': jax.random.normal(ks[8], (I, D), jnp.float32) * s(I, D), 'sw2': jax.random.normal(ks[9], (I, D), jnp.float32) * s(I, D), 'sw3': jax.random.normal(ks[10], (D, I), jnp.float32) * s(D, I)}
    _L0_ffn_all = _L0_ffn_setup()
    _L0_ffn_in = {k: v for k, v in _L0_ffn_all.items() if k in ('gate_w', 'w1', 'b1', 'w2', 'b2', 'w3', 'b3', 'sw1', 'sw2', 'sw3')}
    del _L0_ffn_all
    return {'x': x, 'ctx_1024': ctx_1024, 'mask_BxSxS2_bk1': mask_BxSxS2_bk1, 'g_xattn': g_xattn, 'g_ffn': g_ffn, 'L0_xattn_wq': _L0_xattn_in['wq'], 'L0_xattn_bq': _L0_xattn_in['bq'], 'L0_xattn_wk': _L0_xattn_in['wk'], 'L0_xattn_bk': _L0_xattn_in['bk'], 'L0_xattn_wv': _L0_xattn_in['wv'], 'L0_xattn_bv': _L0_xattn_in['bv'], 'L0_xattn_wo': _L0_xattn_in['wo'], 'L0_xattn_bo': _L0_xattn_in['bo'], 'L0_ffn_gate_w': _L0_ffn_in['gate_w'], 'L0_ffn_w1': _L0_ffn_in['w1'], 'L0_ffn_b1': _L0_ffn_in['b1'], 'L0_ffn_w2': _L0_ffn_in['w2'], 'L0_ffn_b2': _L0_ffn_in['b2'], 'L0_ffn_w3': _L0_ffn_in['w3'], 'L0_ffn_b3': _L0_ffn_in['b3'], 'L0_ffn_sw1': _L0_ffn_in['sw1'], 'L0_ffn_sw2': _L0_ffn_in['sw2'], 'L0_ffn_sw3': _L0_ffn_in['sw3']}

def reference(x, ctx_1024, mask_BxSxS2_bk1, g_xattn, g_ffn, L0_xattn_wq, L0_xattn_bq, L0_xattn_wk, L0_xattn_bk, L0_xattn_wv, L0_xattn_bv, L0_xattn_wo, L0_xattn_bo, L0_ffn_gate_w, L0_ffn_w1, L0_ffn_b1, L0_ffn_w2, L0_ffn_b2, L0_ffn_w3, L0_ffn_b3, L0_ffn_sw1, L0_ffn_sw2, L0_ffn_sw3):
    import jax
    import jax.numpy as jnp

    def _L0_xattn_ref(q, k, v, mask, wq, bq, wk, bk, wv, bv, wo, bo):
        import jax, jax.numpy as jnp
        import numpy as np
        HEADS = 16
        D_MODEL = 128
        D_HEAD = D_MODEL // HEADS

        def _split_head(x):
            B, S, _ = x.shape
            return x.reshape(B, S, HEADS, D_HEAD).transpose(0, 2, 1, 3)
        qh = _split_head(q @ wq.T + bq) * D_HEAD ** (-0.5)
        kh = _split_head(k @ wk.T + bk)
        vh = _split_head(v @ wv.T + bv)
        scores = jnp.einsum('bhqd,bhkd->bhqk', qh, kh)
        scores = jnp.where(mask[:, None, :, :], -1e+20, scores)
        weights = jax.nn.softmax(scores, axis=-1)
        ctx = jnp.einsum('bhqk,bhkd->bhqd', weights, vh)
        B, H, S, D = ctx.shape
        ctx = ctx.transpose(0, 2, 1, 3).reshape(B, S, H * D)
        return ctx @ wo.T + bo

    def _L0_ffn_ref(x, gate_w, w1, b1, w2, b2, w3, b3, sw1, sw2, sw3):
        import jax, jax.numpy as jnp
        import numpy as np
        D = 128
        H = 128
        E = 8
        K = 2
        I = 2 * 128
        ROUTE_SCALE = 1.0
        B, S, _ = x.shape
        xt = x.reshape(-1, D)
        logits = xt @ gate_w.T
        scores = jax.nn.softmax(logits.astype(jnp.float32), axis=-1)
        top_vals, idx = jax.lax.top_k(scores, K)
        weights = jnp.take_along_axis(scores, idx, axis=1).astype(x.dtype) * ROUTE_SCALE
        xs = xt[:, None, :] * weights[:, :, None]
        y = jnp.zeros_like(xt)
        for e in range(E):
            mask = (idx == e).astype(x.dtype)
            h = jax.nn.silu(jnp.einsum('tkd,hd->tkh', xs, w1[e]) + b1[e])
            x2 = jnp.einsum('tkh,dh->tkd', h, w2[e]) + b2[e]
            x3 = jnp.einsum('tkd,hd->tkh', xs, w3[e]) + b3[e]
            y = y + jnp.sum(x2 * x3 * mask[:, :, None], axis=1)
        z = jax.nn.silu(xt @ sw1.T) * (xt @ sw2.T) @ sw3.T
        return (y + z).reshape(B, S, D)
    x = x + jnp.tanh(g_xattn[0]) * _L0_xattn_ref(_layernorm(x, axis=-1), ctx_1024, ctx_1024, mask_BxSxS2_bk1, L0_xattn_wq, L0_xattn_bq, L0_xattn_wk, L0_xattn_bk, L0_xattn_wv, L0_xattn_bv, L0_xattn_wo, L0_xattn_bo)
    x = x + jnp.tanh(g_ffn[0]) * _L0_ffn_ref(_layernorm(x, axis=-1), L0_ffn_gate_w, L0_ffn_w1, L0_ffn_b1, L0_ffn_w2, L0_ffn_b2, L0_ffn_w3, L0_ffn_b3, L0_ffn_sw1, L0_ffn_sw2, L0_ffn_sw3)
    return x

_drawn_inputs = setup_inputs


def setup_inputs(seed=0):
    import zlib

    import numpy as np

    out = dict(_drawn_inputs(seed))
    spreads = {'L0_xattn_bq': (0.0, 0.353),
     'L0_xattn_bk': (0.0, 2.0),
     'L0_xattn_bv': (0.0, 0.1),
     'L0_xattn_bo': (0.0, 0.1)}
    factors = {'L0_ffn_b1': 33.491, 'L0_ffn_b2': 8.0, 'L0_ffn_b3': 28.885}
    for name, (base, spread) in spreads.items():
        noise = np.random.default_rng([zlib.crc32(name.encode()), seed]).standard_normal(out[name].shape)
        drawn = base * np.exp(spread * noise) if base else spread * noise
        out[name] = jnp.asarray(drawn.astype(out[name].dtype))
    for name, factor in factors.items():
        out[name] = (out[name] * factor).astype(out[name].dtype)
    return out
```

```python
from contextlib import ExitStack

import concourse.bass as bass
from concourse import mybir

F32 = mybir.dt.float32
BF16 = mybir.dt.bfloat16
U8 = mybir.dt.uint8
U32 = mybir.dt.uint32
ACT = mybir.ActivationFunctionType
ALU = mybir.AluOpType
AX = mybir.AxisListType

B, S, D = 128, 64, 128
HEADS, DH = 16, 8
E = 8
P = 128
CHUNK = 512
NC = B * S // CHUNK
CB = CHUNK // S
CT = CHUNK // P
G, PR, J = 4, 2, 2
VW = DH + 1
SHARED = 2
XS = 3
NSTEP = CB // 2
ROWS = 6 * E
EPS = 1e-5
MASKED = -1e20

C_IDENT = 0
C_IDUP = C_IDENT + P
C_HEADM = C_IDUP + S
C_OWN = C_HEADM + G
C_IOTA = C_OWN + J
C_IDUPQ = C_IOTA + E
C_SELW = C_IDUPQ + P
C_PART = C_SELW + E * P
C_ROWE = C_PART + 3
C_END = C_ROWE + E

SC0, WB0, G1B, G3B, X2B, WB1, YB = 0, 2, 3, 4, 5, 6, 7


def at(chunk, per_chunk, k):
    return chunk * per_chunk + k


def later(chunk):
    return not (isinstance(chunk, int) and chunk == 0)


def build(nc, x, ctxT, mask, g_x, g_f, wqT, wkT, wvT, woT, bq, bk, bv, bo, gateT, w1T, w2T, w3T,
          b1T, b2T, b3, sw1T, sw2T, sw3T, consts, out):
    with ExitStack() as ctx:
        def sb(name, shape, dt=F32):
            return ctx.enter_context(nc.sbuf_tensor(name, shape, dt))

        def sem(name):
            return ctx.enter_context(nc.semaphore(name))

        cst = sb("cst", [P, C_END])
        ident = cst[:, C_IDENT:C_IDENT + P]
        idup = cst[:, C_IDUP:C_IDUP + S]
        headm = cst[:, C_HEADM:C_HEADM + G]
        own = cst[:, C_OWN:C_OWN + J]
        iota = cst[:, C_IOTA:C_IOTA + E]
        ident_bf = sb("ident_bf", [P, P], BF16)
        idupq_bf = sb("idupq_bf", [S, P], BF16)
        selw = sb("selw", [P, E, P], BF16)
        b3sel = sb("b3sel", [P, E, P], BF16)
        b3row = sb("b3row", [P, P])
        b3part = sb("b3part", [P, 3, P], BF16)
        b3rest = sb("b3rest", [P, P])
        b3pick = sb("b3pick", [P, 2, P])
        wq_s, wk_s = sb("wq_s", [P, D]), sb("wk_s", [P, D])
        wv_s, wo_s = sb("wv_s", [P, PR, D // 2]), sb("wo_s", [P, D])
        gate_s = sb("gate_s", [P, E])
        w1_s, w2_s, w3_s = (sb(n, [P, E, P]) for n in ("w1_s", "w2_s", "w3_s"))
        sw1_s, sw2_s, sw3_s = (sb(n, [P, SHARED, P]) for n in ("sw1_s", "sw2_s", "sw3_s"))
        b1_s, b2_s = sb("b1_s", [P, E]), sb("b2_s", [P, E])
        bq_s, bk_s, bv_s = (sb(n, [P, 1]) for n in ("bq_s", "bk_s", "bv_s"))
        bqm = sb("bqm", [P, G])
        bo_s = sb("bo_s", [P, D])
        gx_s, gf_s = sb("gx_s", [P, 1]), sb("gf_s", [P, 1])
        tgx, tgf = sb("tgx", [P, 1]), sb("tgf", [P, 1])
        pow_s, eps_s = sb("pow_s", [P, CT]), sb("eps_s", [P, CT])

        xin = sb("xin", [P, CT, D])
        cT = sb("cT", [P, CHUNK])
        mk8 = sb("mk8", [S, CB, S], U8)
        mkneg = sb("mkneg", [S, CB, S], BF16)
        bn1, bn2 = sb("bn1", [P, CT, 6]), sb("bn2", [P, CT, 6])
        mv1, mv2 = sb("mv1", [P, CT, 2]), sb("mv2", [P, CT, 2])
        ve1, ve2 = sb("ve1", [P, CT]), sb("ve2", [P, CT])
        rs1, rs2 = sb("rs1", [P, CT]), sb("rs2", [P, CT])
        xn1, xn2 = sb("xn1", [P, CT, D]), sb("xn2", [P, CT, D])
        resid = sb("resid", [P, CT, D])
        xT = sb("xT", [P, CHUNK])
        qexp = sb("qexp", [P, CB, G, S])
        kexp = sb("kexp", [P, G, CHUNK])
        vexp = sb("vexp", [P, CB, G, PR * J * VW])
        smax = sb("smax", [P, 2, PR * G])
        pr = sb("pr", [P, CB, G, PR * S])
        prT = sb("prT", [P, CB, G, P])
        rden = sb("rden", [P, 2, CB // 2, HEADS])
        rown = sb("rown", [P, 2, CB // 2, HEADS])
        on = sb("on", [P, CB, D])
        oT = sb("oT", [P, CHUNK])
        x1 = sb("x1", [P, CT, D])
        x2T = sb("x2T", [P, CHUNK])
        lmax, lsum, lrec = sb("lmax", [P, CT]), sb("lsum", [P, CT]), sb("lrec", [P, CT])
        lsub, lexp, score = (sb(n, [P, CT, E]) for n in ("lsub", "lexp", "score"))
        top8 = sb("top8", [P, CT, 8])
        topi = sb("topi", [P, CT, 8], U32)
        topf = sb("topf", [P, CT, 2])
        is0, is1 = sb("is0", [P, CT, E]), sb("is1", [P, CT, E])
        wsel, wr1, wr2 = (sb(n, [P, CT, E]) for n in ("wsel", "wr1", "wr2"))
        wm = sb("wm", [P, CT, P], BF16)
        wmT = sb("wmT", [P, CHUNK], BF16)
        sa = sb("sa", [P, SHARED, CHUNK])
        sh = sb("sh", [P, SHARED, CHUNK])
        xs = sb("xs", [P, XS, CHUNK])
        hb = sb("hb", [P, 2, CHUNK])
        x3 = sb("x3", [P, 2, CHUNK])
        prod = sb("prod", [P, 4, CHUNK])
        yacc = sb("yacc", [P, CHUNK])
        ob = sb("ob", [P, CT, D])

        ps = ctx.enter_context(nc.psum_tensor("ps", [P, 8, 512], F32))

        s_cst = sem("weights_loaded")
        s_set = sem("setup_step")
        s_ready = sem("setup_ready")
        s_pset = sem("pool_setup")
        s_tanh = sem("tanh_ready")
        s_x, s_ctx, s_mk, s_st = sem("x_loaded"), sem("ctx_loaded"), sem("mask_loaded"), sem("out_stored")
        s_stat1, s_stat2 = sem("ln1_moments"), sem("ln2_moments")
        s_rs2 = sem("ln2_rstd")
        s_pstep, v_step = sem("pool_own_step"), sem("dve_own_step")
        s_mneg, s_xn1, s_res, s_xn2, s_add = (sem(n) for n in (
            "mask_ready", "xn1_ready", "resid_ready", "xn2_ready", "expert_added"))
        p_pt, p_pv, p_ot, p_ao, p_xt, p_q, p_k, p_v = (sem(n) for n in (
            "pe_probsT", "pe_pv", "pe_oT", "pe_attn_out", "pe_xT", "pe_q", "pe_k", "pe_v"))
        p_x2t, p_gate, p_s, p_sa, p_sb, p_wmt = (sem(n) for n in (
            "pe_x2T", "pe_gate", "pe_scores", "pe_shared1", "pe_shared2", "pe_routeT"))
        p_wb, p_g1, p_g3, p_x2, p_y = (sem(n) for n in (
            "pe_weight_rows", "pe_w1", "pe_w3", "pe_w2", "pe_y"))
        a_exp, a_pt, a_ot, a_xt, a_q, a_x2t, a_ge = (sem(n) for n in (
            "act_probs", "act_probsT", "act_oT", "act_xT", "act_q", "act_x2T", "act_gate_exp"))
        a_sa, a_h, a_x3 = (sem(n) for n in ("act_shared", "act_h", "act_x3"))
        v_pt, v_k, v_v, v_max, v_sub, v_rec, v_norm, v_x1 = (sem(n) for n in (
            "dve_probsT", "dve_k", "dve_v", "dve_max", "dve_scores_shifted", "dve_sum_recip",
            "dve_o_normed", "dve_x1"))
        v_lmax, v_lsub, v_wm, v_wmt, v_sh, v_xs, v_prod, v_out = (sem(n) for n in (
            "dve_logit_max", "dve_logits_shifted", "dve_routes", "dve_routeT",
            "dve_shared", "dve_xs", "dve_prod", "dve_out"))

        def bc(ap, axis, n):
            ap = ap.unsqueeze(axis)
            shape = list(ap.shape)
            shape[axis] = n
            return ap.broadcast_to(shape)

        block = ctx.enter_context(nc.Block())

        @block.sync
        def _(sp):
            loads = [
                (cst[:, :], consts), (gx_s[:, :], g_x.partition_broadcast(P)),
                (gf_s[:, :], g_f.partition_broadcast(P)), (bo_s[:, :], bo.partition_broadcast(P)),
                (wq_s[:, :], wqT), (wk_s[:, :], wkT), (wv_s[:, :, :], wvT), (wo_s[:, :], woT),
                (bq_s[:, :], bq), (bk_s[:, :], bk), (bv_s[:, :], bv), (gate_s[:, :], gateT),
                (b1_s[:, :], b1T), (b2_s[:, :], b2T)]
            loads += [(b3row[E * r:E * r + E, :], b3) for r in range(P // E)]
            loads += [(sw1_s[:, :, :], sw1T), (sw2_s[:, :, :], sw2T), (sw3_s[:, :, :], sw3T),
                      (w1_s[:, :, :], w1T), (w2_s[:, :, :], w2T), (w3_s[:, :, :], w3T)]
            assert len(loads) == N_LOADS

            def load_x(t):
                if later(t):
                    sp.wait_ge(s_xn1, t)
                    sp.wait_ge(s_res, t)
                sp.dma_start(xin[:, :, :], x[t].rearrange("p (t d) -> p t d", t=CT)).then_inc(s_x, 16)

            def load_ctx(t):
                if later(t):
                    sp.wait_ge(p_v, t)
                    sp.wait_ge(s_mneg, t)
                sp.dma_start(cT[:, :], ctxT[t]).then_inc(s_ctx, 16)
                sp.dma_start(mk8[:, :, :], mask[t].rearrange("q (b k) -> q b k", b=CB)).then_inc(s_mk, 16)

            def store(c):
                sp.wait_ge(v_out, at(c, 1, 1))
                sp.dma_start(out[c].rearrange("p (t d) -> p t d", t=CT), ob[:, :, :]).then_inc(s_st, 16)

            load_x(0)
            for dst, src in loads:
                sp.dma_start(dst, src).then_inc(s_cst, 16)
            load_ctx(0)
            load_x(1)
            load_ctx(1)
            load_x(2)
            load_ctx(2)
            store(0)
            with sp.Fori(2, NC - 1) as t:
                c = sp.snap(t - 1)
                load_x(t + 1)
                load_ctx(t + 1)
                store(c)
            store(NC - 2)
            store(NC - 1)
            sp.wait_ge(s_st, 16 * NC)

        @block.gpsimd
        def _(pool):
            pool.memset(vexp[:, :, :, :], 0.0).then_inc(s_pset, 1)
            pool.memset(kexp[:, :, :], 0.0).then_inc(s_pset, 1)
            pool.memset(pow_s[:, :], -0.5).then_inc(s_pset, 1)
            pool.memset(eps_s[:, :], EPS).then_inc(s_pset, 1)
            pool.memset(wm[:, :, :], 0.0).then_inc(s_pset, 1)
            pool.wait_ge(s_pset, 5)
            for pair in range(PR):
                ones = vexp[S * pair:S * pair + S, :, :, :].rearrange("q b g (p j n) -> q (b g) p j n", p=PR, j=J)
                pool.memset(ones[:, :, pair, :, DH], 1.0).then_inc(s_pset, 1)

            def rstd(stat, k, ve, rs, mv):
                pool.wait_ge(stat, at(k, 1, 1))
                pool.tensor_tensor(ve[:, :], mv[:, :, 1], eps_s[:, :], ALU.add).then_inc(s_pstep, 1)
                pool.wait_ge(s_pstep, 1)
                return pool.tensor_tensor(rs[:, :], ve[:, :], pow_s[:, :], ALU.pow)

            def front(t):
                pool.sem_clear(s_pstep)
                pool.wait_ge(s_x, at(t, 16, 16))
                if later(t):
                    pool.wait_ge(p_xt, t)
                pool.wait_ge(s_mk, at(t, 16, 16))
                if later(t):
                    pool.wait_ge(p_s, at(t, NSTEP, 0))
                rstd(s_stat1, t, ve1, rs1, mv1).then_inc(s_pstep, 1)
                pool.wait_ge(s_pstep, 2)
                for i in range(CT):
                    last = pool.tensor_scalar(xn1[:, i, :], xin[:, i, :], mv1[:, i, 0:1], rs1[:, i:i + 1],
                                              ALU.subtract, ALU.mult)
                last.then_inc(s_xn1, 1)
                pool.tensor_scalar(mkneg[:, :, :], mk8[:, :, :], MASKED, None, ALU.mult).then_inc(s_mneg, 1)

            def keep(t):
                if later(t):
                    pool.wait_ge(v_x1, t)
                pool.tensor_tensor(resid[:, :, :], xin[:, :, :], bc(bo_s[:, :], 1, CT), ALU.add).then_inc(s_res, 1)

            def back(c):
                pool.sem_clear(s_pstep)
                if later(c):
                    pool.wait_ge(s_xn2, c)
                rstd(s_stat2, c, ve2, rs2, mv2).then_inc(s_rs2, 1)

            def experts(c):
                for e in range(1, E):
                    pool.wait_ge(v_prod, at(c, E, e + 1))
                    if e == 1:
                        if later(c):
                            pool.wait_ge(p_y, c)
                        first = prod[:, 0, :]
                    else:
                        pool.wait_ge(s_add, at(c, E - 1, e - 1))
                        first = yacc[:, :]
                    pool.tensor_tensor(yacc[:, :], first, prod[:, e % 4, :], ALU.add).then_inc(s_add, 1)

            pool.wait_ge(s_ready, 1)
            front(0)
            keep(0)

            def step(t):
                front(t)
                back(t - 1)
                keep(t)
                experts(t - 1)

            step(1)
            with pool.Fori(2, NC) as t:
                step(t)
            back(NC - 1)
            experts(NC - 1)

        @block.scalar
        def _(act):
            act.wait_ge(s_cst, 16 * N_LOADS)
            act.activation(tgx[:, :], gx_s[:, :], ACT.Tanh).then_inc(s_tanh, 1)
            act.activation(tgf[:, :], gf_s[:, :], ACT.Tanh).then_inc(s_tanh, 1)
            act.wait_ge(s_ready, 1)

            def probs(c, n):
                act.wait_ge(v_sub, at(c, NSTEP, n + 1))
                p2 = pr[:, 2 * n:2 * n + 2, :, :].rearrange("q b g k -> q (b g k)")
                act.activation(p2, p2, ACT.Exp).then_inc(a_exp, 1)

            def probs_t(c, b):
                act.wait_ge(p_pt, at(c, CB, b + 1))
                if later(c):
                    act.wait_ge(p_pv, at(c, 2, 0))
                act.activation(prT[:, b, :, :].rearrange("p g q -> p (g q)"), ps[:, G1B, :], ACT.Copy).then_inc(a_pt, 1)

            def probs_all(c):
                probs(c, 0)
                probs(c, 1)
                probs_t(c, 0)
                probs(c, 2)
                probs_t(c, 2)
                probs(c, 3)
                probs_t(c, 4)
                probs_t(c, 6)

            def o_t(c):
                act.wait_ge(p_ot, at(c, 1, 1))
                if later(c):
                    act.wait_ge(p_ao, c)
                act.activation(oT[:, :], ps[:, WB0, :], ACT.Identity, bias=bv_s[:, :]).then_inc(a_ot, 1)

            def x_t(t):
                act.wait_ge(p_xt, at(t, 1, 1))
                if later(t):
                    act.wait_ge(p_q, t)
                act.activation(xT[:, :], ps[:, WB1, :], ACT.Copy).then_inc(a_xt, 1)

            def queries(t):
                act.wait_ge(p_q, at(t, 1, 1))
                if later(t):
                    act.wait_ge(p_s, at(t, NSTEP, 0))
                for m in range(G):
                    last = act.activation(qexp[:, :, m, :], ps[:, YB, :].rearrange("p (b q) -> p b q", q=S), ACT.Identity, bias=bqm[:, m:m + 1],
                                          scale=headm[:, m:m + 1])
                last.then_inc(a_q, 1)

            def gate(c):
                act.wait_ge(p_x2t, at(c, 1, 1))
                if later(c):
                    act.wait_ge(p_gate, c)
                    act.wait_ge(p_sb, at(c, SHARED, 0))
                    act.wait_ge(v_xs, at(c, E, 0))
                act.activation(x2T[:, :], ps[:, WB0, :], ACT.Copy).then_inc(a_x2t, 1)
                act.wait_ge(v_lsub, at(c, 1, 1))
                act.activation(lexp[:, :, :], lsub[:, :, :], ACT.Exp).then_inc(a_ge, 1)

            def experts(c):
                for m in range(SHARED):
                    act.wait_ge(p_sa, at(c, SHARED, m + 1))
                    if later(c):
                        act.wait_ge(v_sh, at(c, SHARED, 0))
                    act.activation(sa[:, m, :], ps[:, G1B, :], ACT.Silu).then_inc(a_sa, 1)
                for e in range(E):
                    act.wait_ge(p_g1, at(c, E, e + 1))
                    if e >= 2:
                        act.wait_ge(p_x2, at(c, E, e - 1))
                    act.activation(hb[:, e % 2, :], ps[:, G1B, :], ACT.Silu, bias=b1_s[:, e:e + 1]).then_inc(a_h, 1)
                    act.wait_ge(p_g3, at(c, E, e + 1))
                    if e >= 2:
                        act.wait_ge(v_prod, at(c, E, e - 1))
                    act.activation(x3[:, e % 2, :], ps[:, G3B, :], ACT.Copy).then_inc(a_x3, 1)

            x_t(0)
            queries(0)

            def step(t):
                probs_all(t - 1)
                x_t(t)
                o_t(t - 1)
                queries(t)
                gate(t - 1)
                experts(t - 1)

            step(1)
            with act.Fori(2, NC) as t:
                step(t)
            probs_all(NC - 1)
            o_t(NC - 1)
            gate(NC - 1)
            experts(NC - 1)

        @block.vector
        def _(dve):
            dve.wait_ge(s_cst, 16 * N_LOADS)
            step = [0]

            def link(ins):
                step[0] += 1
                ins.then_inc(s_set, 1)
                dve.wait_ge(s_set, step[0])

            dve.wait_ge(s_tanh, 2)
            dve.tensor_scalar(bqm[:, :], headm, bq_s[:, 0:1], None, ALU.mult)
            dve.tensor_copy(ident_bf[:, :], ident)
            dve.tensor_copy(idupq_bf[:, :], cst[0:S, C_IDUPQ:C_IDUPQ + P])
            dve.tensor_copy(selw[:, :, :].rearrange("r e p -> r (e p)"), cst[:, C_SELW:C_SELW + E * P])
            link(dve.tensor_scalar(wo_s[:, :], wo_s[:, :], tgx[:, 0:1], None, ALU.mult))
            link(dve.tensor_scalar(bo_s[:, :], bo_s[:, :], tgx[:, 0:1], None, ALU.mult))
            link(dve.tensor_copy(b3part[:, 0, :], b3row[:, :]))
            link(dve.tensor_tensor(b3rest[:, :], b3row[:, :], b3part[:, 0, :], ALU.subtract))
            link(dve.tensor_copy(b3part[:, 1, :], b3rest[:, :]))
            link(dve.tensor_tensor(b3part[:, 2, :], b3rest[:, :], b3part[:, 1, :], ALU.subtract))
            part = [cst[:, C_PART + k:C_PART + k + 1] for k in range(3)]
            link(dve.tensor_scalar(b3pick[:, 0, :], b3part[:, 0, :], part[0], None, ALU.mult))
            link(dve.scalar_tensor_tensor(b3pick[:, 1, :], b3part[:, 1, :], part[1], b3pick[:, 0, :], ALU.mult, ALU.add))
            link(dve.scalar_tensor_tensor(b3pick[:, 0, :], b3part[:, 2, :], part[2], b3pick[:, 1, :], ALU.mult, ALU.add))
            for e in range(E):
                link(dve.tensor_scalar(b3sel[:, e, :], b3pick[:, 0, :], cst[:, C_ROWE + e:C_ROWE + e + 1],
                                       None, ALU.mult))
            dve.wait_ge(s_pset, 7)
            dve.memset(smax[:, :, :], 0.0).then_inc(s_ready, 1)

            def stats(src, bn, mv, done):
                for i in range(CT):
                    last = dve.bn_stats(bn[:, i, :], src[:, i, :])
                last.then_inc(v_step, 1)
                dve.wait_ge(v_step, 1)
                for i in range(CT):
                    last = dve.bn_aggr(mv[:, i, :], bn[:, i, :])
                last.then_inc(done, 1)

            def front_stats(t):
                dve.sem_clear(v_step)
                dve.wait_ge(s_x, at(t, 16, 16))
                if later(t):
                    dve.wait_ge(s_xn1, t)
                stats(xin, bn1, mv1, s_stat1)

            def probs_t(c, b):
                dve.wait_ge(p_pt, at(c, CB, b + 1))
                if later(c):
                    dve.wait_ge(p_pv, at(c, 2, 0))
                dve.tensor_copy(prT[:, b, :, :].rearrange("p g q -> p (g q)"), ps[:, G3B, :]).then_inc(v_pt, 1)

            def norm(c, h):
                dve.wait_ge(p_pv, at(c, 2, h + 1))
                bank = WB1 if h == 0 else SC0
                o = ps[:, bank:bank + 2, :].rearrange("q n (s w) -> q (n s) w", s=2)[:, :, 0:HEADS * VW].rearrange(
                    "q b (h n) -> q b h n", n=VW)
                dve.reciprocal(rden[:, h, :, :], o[:, :, :, DH]).then_inc(v_rec, 1)
                dve.wait_ge(v_rec, at(c, 4, 2 * h + 1))
                dve.tensor_tensor(rown[:, h, :, :].rearrange("q b (a j) -> q (b a) j", j=J),
                                  rden[:, h, :, :].rearrange("q b (a j) -> q (b a) j", j=J),
                                  bc(own, 1, CB // 2 * HEADS // J), ALU.mult).then_inc(v_rec, 1)
                dve.wait_ge(v_rec, at(c, 4, 2 * h + 2))
                if later(c):
                    dve.wait_ge(p_ot, c)
                n = CB // 2
                dve.tensor_tensor(on[:, n * h:n * h + n, :].rearrange("q b (h d) -> q b h d", d=DH),
                                  o[:, :, :, 0:DH], bc(rown[:, h, :, :], 3, DH), ALU.mult).then_inc(v_norm, 1)

            def attend(c):
                probs_t(c, 1)
                probs_t(c, 3)
                norm(c, 0)
                probs_t(c, 5)
                probs_t(c, 7)
                norm(c, 1)

            def residual(c):
                dve.sem_clear(v_step)
                dve.wait_ge(p_ao, at(c, 1, 1))
                dve.wait_ge(s_res, at(c, 1, 1))
                dve.tensor_tensor(x1[:, :, :], ps[:, X2B, :].rearrange("q (t d) -> q t d", t=CT), resid[:, :, :],
                                  ALU.add).then_inc(v_x1, 1)
                dve.wait_ge(v_x1, at(c, 1, 1))
                stats(x1, bn2, mv2, s_stat2)

            def ln2(c):
                dve.wait_ge(s_rs2, at(c, 1, 1))
                if later(c):
                    dve.wait_ge(p_x2t, c)
                for i in range(CT):
                    last = dve.tensor_scalar(xn2[:, i, :], x1[:, i, :], mv2[:, i, 0:1], rs2[:, i:i + 1],
                                             ALU.subtract, ALU.mult)
                last.then_inc(s_xn2, 1)

            def keys(t):
                dve.wait_ge(p_k, at(t, 1, 1))
                if later(t):
                    dve.wait_ge(p_s, at(t, NSTEP, 0))
                for g in range(G):
                    q = slice(32 * g, 32 * g + 32)
                    last = dve.tensor_scalar(kexp[q, g, :], ps[q, G3B, :], bk_s[q, 0:1], None, ALU.add)
                last.then_inc(v_k, 1)

            def values(t):
                dve.wait_ge(p_v, at(t, 1, 1))
                if later(t):
                    dve.wait_ge(p_pv, at(t, 2, 0))
                for pair in range(PR):
                    q = slice(S * pair, S * pair + S)
                    dst = vexp[q, :, :, :].rearrange("q b g (p j n) -> q (b g) p j n", p=PR, j=J)
                    last = dve.tensor_copy(dst[:, :, pair, :, 0:DH],
                                           ps[q, G1B, :].rearrange("q (a j n) -> q a j n", j=J, n=DH))
                last.then_inc(v_v, 1)

            def gate_max(c):
                logit = ps[:, X2B, 0:CT * E].rearrange("q (t e) -> q t e", e=E)
                dve.wait_ge(p_gate, at(c, 1, 1))
                dve.reduce_max(lmax[:, :], logit, AX.X).then_inc(v_lmax, 1)
                dve.wait_ge(v_lmax, at(c, 1, 1))
                dve.tensor_tensor(lsub[:, :, :], logit, bc(lmax[:, :], 2, E), ALU.subtract).then_inc(v_lsub, 1)

            def route(c):
                n = [0]

                def link(ins):
                    n[0] += 1
                    ins.then_inc(v_step, 1)
                    dve.wait_ge(v_step, n[0])

                dve.sem_clear(v_step)
                dve.wait_ge(a_ge, at(c, 1, 1))
                link(dve.reduce_sum(lsum[:, :], lexp[:, :, :], AX.X))
                link(dve.reciprocal(lrec[:, :], lsum[:, :]))
                link(dve.tensor_tensor(score[:, :, :], lexp[:, :, :], bc(lrec[:, :], 2, E), ALU.mult))
                for i in range(CT):
                    last = dve.max(top8[:, i, :], score[:, i, :])
                link(last)
                for i in range(CT):
                    last = dve.max_index(topi[:, i, :], top8[:, i, :], score[:, i, :])
                link(last)
                link(dve.tensor_copy(topf[:, :, :], topi[:, :, 0:2]))
                dve.tensor_tensor(is0[:, :, :], bc(iota, 1, CT), bc(topf[:, :, 0], 2, E), ALU.is_equal)
                link(dve.tensor_tensor(is1[:, :, :], bc(iota, 1, CT), bc(topf[:, :, 1], 2, E), ALU.is_equal))
                if later(c):
                    dve.wait_ge(p_wmt, c)
                link(dve.tensor_tensor(is1[:, :, :], is0[:, :, :], is1[:, :, :], ALU.add))
                dve.tensor_copy(wm[:, :, 3 * E:ROWS].rearrange("q t (r e) -> q t r e", r=3), bc(is1[:, :, :], 2, 3))
                link(dve.tensor_tensor(wsel[:, :, :], score[:, :, :], is1[:, :, :], ALU.mult))
                link(dve.tensor_copy(wm[:, :, 0:E], wsel[:, :, :]))
                link(dve.tensor_tensor(wr1[:, :, :], wsel[:, :, :], wm[:, :, 0:E], ALU.subtract))
                link(dve.tensor_copy(wm[:, :, E:2 * E], wr1[:, :, :]))
                dve.tensor_tensor(wm[:, :, 2 * E:3 * E], wr1[:, :, :], wm[:, :, E:2 * E],
                                  ALU.subtract).then_inc(v_wm, 1)

            def scores(t, n):
                s4 = ps[:, SC0:SC0 + 2, :].rearrange("q b (a k) -> q (b a) k", k=S)
                dve.wait_ge(p_s, at(t, NSTEP, n + 1))
                dve.reduce_max(smax[:, :, :].rearrange("q b a -> q (b a)"), s4, AX.X).then_inc(v_max, 1)
                dve.wait_ge(v_max, at(t, NSTEP, n + 1))
                if later(t):
                    dve.wait_ge(p_pt, at(t, CB, 0))
                dve.tensor_tensor(pr[:, 2 * n:2 * n + 2, :, :].rearrange("q b g (p k) -> q (b g p) k", k=S), s4,
                                  bc(smax[:, :, :].rearrange("q b a -> q (b a)"), 2, S),
                                  ALU.subtract).then_inc(v_sub, 1)

            def shared(c, m):
                dve.wait_ge(a_sa, at(c, SHARED, m + 1))
                dve.wait_ge(p_sb, at(c, SHARED, m + 1))
                if later(c):
                    dve.wait_ge(p_y, c)
                dve.tensor_tensor(sh[:, m, :], ps[:, G3B, :], sa[:, m, :], ALU.mult).then_inc(v_sh, 1)

            def scale_x(c, e):
                dve.wait_ge(p_wb, at(c, E, e + 1))
                if e >= XS:
                    dve.wait_ge(p_g3, at(c, E, e - XS + 1))
                dve.tensor_tensor(xs[:, e % XS, :], ps[:, WB1 if e % 2 else WB0, :], x2T[:, :],
                                  ALU.mult).then_inc(v_xs, 1)

            def combine(c, e):
                dve.wait_ge(p_x2, at(c, E, e + 1))
                dve.wait_ge(a_x3, at(c, E, e + 1))
                if e >= 4:
                    dve.wait_ge(s_add, at(c, E - 1, max(e - 4, 1)))
                elif later(c):
                    dve.wait_ge(s_add, at(c, E - 1, 0))
                dve.scalar_tensor_tensor(prod[:, e % 4, :], ps[:, X2B, :], b2_s[:, e:e + 1], x3[:, e % 2, :],
                                         ALU.add, ALU.mult).then_inc(v_prod, 1)

            def ffn(c, t):
                if t is not None:
                    scores(t, 0)
                route(c)
                shared(c, 0)
                if t is not None:
                    scores(t, 1)
                shared(c, 1)
                dve.wait_ge(p_wmt, at(c, 1, 1))
                if later(c):
                    dve.wait_ge(p_g3, at(c, E, 0))
                dve.tensor_copy(wmT[:, :], ps[:, WB1, 0:CHUNK // 2].bitcast(BF16)).then_inc(v_wmt, 1)
                scale_x(c, 0)
                scale_x(c, 1)
                for e in range(E):
                    if e + 2 < E:
                        scale_x(c, e + 2)
                    combine(c, e)
                    if t is not None and e in SCORE_AT:
                        scores(t, SCORE_AT.index(e) + 2)
                dve.wait_ge(p_y, at(c, 1, 1))
                if later(c):
                    dve.wait_ge(s_st, at(c, 16, 0))
                dve.scalar_tensor_tensor(ob[:, :, :].rearrange("q t d -> q (t d)"), ps[:, YB, :], tgf[:, 0:1],
                                         x1[:, :, :].rearrange("q t d -> q (t d)"), ALU.mult, ALU.add).then_inc(v_out, 1)

            front_stats(0)
            keys(0)
            values(0)
            for n in range(NSTEP):
                scores(0, n)

            def step(t):
                front_stats(t)
                attend(t - 1)
                keys(t)
                residual(t - 1)
                values(t)
                ln2(t - 1)
                gate_max(t - 1)
                ffn(t - 1, t)

            step(1)
            with dve.Fori(2, NC) as t:
                step(t)
            attend(NC - 1)
            residual(NC - 1)
            ln2(NC - 1)
            gate_max(NC - 1)
            ffn(NC - 1, None)

        @block.tensor
        def _(pe):
            def probs_t(c, b):
                pe.wait_ge(a_exp, at(c, NSTEP, b // 2 + 1))
                if b == 0:
                    if later(c):
                        pe.wait_ge(a_h, at(c, E, 0))
                elif b == 1:
                    if later(c):
                        pe.wait_ge(a_x3, at(c, E, 0))
                elif b % 2 == 0:
                    pe.wait_ge(a_pt, at(c, CB // 2, b // 2))
                else:
                    pe.wait_ge(v_pt, at(c, CB // 2, b // 2))
                bank = G3B if b % 2 else G1B
                for g in range(G):
                    last = pe.transpose(ps[:, bank, g * P:g * P + P], pr[:, b, g, :], ident)
                last.then_inc(p_pt, 1)

            def pv(c, b):
                if b == 0:
                    if later(c):
                        pe.wait_ge(v_xs, at(c, E, 0))
                        pe.wait_ge(v_out, c)
                if b == CB // 2:
                    pe.wait_ge(v_sub, at(c, NSTEP, NSTEP))
                if b % 2:
                    pe.wait_ge(v_pt, at(c, CB // 2, b // 2 + 1))
                else:
                    pe.wait_ge(a_pt, at(c, CB // 2, b // 2 + 1))
                bank = WB1 if b < CB // 2 else SC0
                i = b % (CB // 2)
                for g in range(G):
                    w = PR * J * VW
                    last = pe.matmul(ps[:, bank + i // 2, 256 * (i % 2) + w * g:256 * (i % 2) + w * g + w],
                                     prT[:, b, g, :], vexp[:, b, g, :], start=True, stop=True)
                if i == CB // 2 - 1:
                    last.then_inc(p_pv, 1)

            def attend(c):
                for b in range(CB + 1):
                    if b < CB:
                        probs_t(c, b)
                    if b:
                        pv(c, b - 1)

            def o_t(c):
                for b in range(CB):
                    if b % (CB // 2) == 0:
                        pe.wait_ge(v_norm, at(c, 2, b // (CB // 2) + 1))
                    last = pe.matmul(ps[:, WB0, S * b:S * b + S], on[:, b, :], idup, start=True, stop=True)
                last.then_inc(p_ot, 1)

            def attn_out(c):
                pe.wait_ge(a_ot, at(c, 1, 1))
                if later(c):
                    pe.wait_ge(v_prod, at(c, E, 0))
                for i in range(CT):
                    last = pe.matmul(ps[:, X2B, P * i:P * i + P], oT[:, P * i:P * i + P], wo_s[:, :],
                                     start=True, stop=True)
                last.then_inc(p_ao, 1)

            def x_t(t):
                pe.wait_ge(s_xn1, at(t, 1, 1))
                if later(t):
                    pe.wait_ge(v_norm, at(t - 1, 2, 1))
                for i in range(CT):
                    last = pe.transpose(ps[:, WB1, P * i:P * i + P], xn1[:, i, :], ident)
                last.then_inc(p_xt, 1)

            def queries(t):
                pe.wait_ge(a_xt, at(t, 1, 1))
                pe.matmul(ps[:, YB, :], wq_s[:, :], xT[:, :], start=True, stop=True).then_inc(p_q, 1)

            def keys(t):
                pe.wait_ge(s_ctx, at(t, 16, 16))
                if later(t):
                    pe.wait_ge(v_pt, at(t, CB // 2, 0))
                pe.matmul(ps[:, G3B, :], wk_s[:, :], cT[:, :], start=True, stop=True).then_inc(p_k, 1)

            def values(t):
                if later(t):
                    pe.wait_ge(a_pt, at(t, CB // 2, 0))
                for b in range(CB):
                    for pair in range(PR):
                        last = pe.matmul(ps[S * pair:S * pair + S, G1B, S * b:S * b + S], cT[:, S * b:S * b + S],
                                         wv_s[:, pair, :], start=True, stop=True)
                last.then_inc(p_v, 1)

            def scores(t, n):
                if n == 0:
                    pe.wait_ge(a_q, at(t, 1, 1))
                    pe.wait_ge(v_k, at(t, 1, 1))
                    if later(t):
                        pe.wait_ge(v_norm, at(t, 2, 0))
                    pe.wait_ge(s_mneg, at(t, 1, 1))
                if later(t) or n:
                    pe.wait_ge(v_sub, at(t, NSTEP, n))
                for i in range(2):
                    b = 2 * n + i
                    pe.matmul(ps[:, SC0 + i, :].rearrange("q (a k) -> q a k", k=S), idupq_bf[:, :],
                              bc(mkneg[:, b, :], 1, PR * G), start=True, stop=False)
                    for pair in range(PR):
                        last = pe.matmul(ps[:, SC0 + i, :].rearrange("q (g p k) -> q g p k", g=G, p=PR)[:, :, pair, :],
                                         qexp[:, b, 2 * pair:2 * pair + 2, :].rearrange("f m q -> f (m q)"),
                                         kexp[:, :, S * b:S * b + S], start=False, stop=(pair == PR - 1))
                last.then_inc(p_s, 1)

            def gate(c):
                pe.wait_ge(s_xn2, at(c, 1, 1))
                for i in range(CT):
                    last = pe.transpose(ps[:, WB0, P * i:P * i + P], xn2[:, i, :], ident)
                last.then_inc(p_x2t, 1)
                pe.wait_ge(a_x2t, at(c, 1, 1))
                pe.wait_ge(v_x1, at(c, 1, 1))
                for i in range(CT):
                    last = pe.matmul(ps[:, X2B, E * i:E * i + E], x2T[:, P * i:P * i + P], gate_s[:, :],
                                     start=True, stop=True)
                last.then_inc(p_gate, 1)

            def shared(c, m, t):
                if m:
                    pe.wait_ge(a_sa, at(c, SHARED, m))
                elif t is not None:
                    pe.wait_ge(v_v, at(t, 1, 1))
                    pe.wait_ge(v_k, at(t, 1, 1))
                else:
                    pe.wait_ge(a_pt, at(c, CB // 2, CB // 2))
                    pe.wait_ge(v_pt, at(c, CB // 2, CB // 2))
                pe.matmul(ps[:, G1B, :], sw1_s[:, m, :], x2T[:, :], start=True, stop=True).then_inc(p_sa, 1)
                if m:
                    pe.wait_ge(v_sh, at(c, SHARED, m))
                pe.matmul(ps[:, G3B, :], sw2_s[:, m, :], x2T[:, :], start=True, stop=True).then_inc(p_sb, 1)

            def weight_rows(c, e):
                if e == 1:
                    pe.wait_ge(v_wmt, at(c, 1, 1))
                if e >= 2:
                    pe.wait_ge(v_xs, at(c, E, e - 1))
                pe.matmul(ps[:, WB1 if e % 2 else WB0, :], selw[:, e, :], wmT[:, :], start=True,
                          stop=True).then_inc(p_wb, 1)

            def up(c, e):
                pe.wait_ge(v_xs, at(c, E, e + 1))
                if e:
                    pe.wait_ge(a_h, at(c, E, e))
                else:
                    pe.wait_ge(a_sa, at(c, SHARED, SHARED))
                pe.matmul(ps[:, G1B, :], w1_s[:, e, :], xs[:, e % XS, :], start=True, stop=True).then_inc(p_g1, 1)
                if e:
                    pe.wait_ge(a_x3, at(c, E, e))
                else:
                    pe.wait_ge(v_sh, at(c, SHARED, SHARED))
                pe.matmul(ps[:, G3B, :], b3sel[:, e, :], wmT[:, :], start=True, stop=False)
                pe.matmul(ps[:, G3B, :], w3_s[:, e, :], xs[:, e % XS, :], start=False, stop=True).then_inc(p_g3, 1)

            def down(c, e):
                pe.wait_ge(a_h, at(c, E, e + 1))
                if e:
                    pe.wait_ge(v_prod, at(c, E, e))
                else:
                    pe.wait_ge(v_wm, at(c, 1, 1))
                pe.matmul(ps[:, X2B, :], w2_s[:, e, :], hb[:, e % 2, :], start=True, stop=True).then_inc(p_x2, 1)

            def shared_down(c, m):
                pe.wait_ge(v_sh, at(c, SHARED, m + 1))
                for i in range(CT):
                    q = slice(P * i, P * i + P)
                    pe.matmul(ps[:, YB, q], sh[:, m, q], sw3_s[:, m, :], start=(m == 0 and i == 0), stop=False,
                              skip_group_check=True)

            def ffn(c, t):
                shared(c, 0, t)
                if t is not None:
                    scores(t, 1)
                shared(c, 1, t)
                pe.wait_ge(v_wm, at(c, 1, 1))
                for i in range(CT):
                    last = pe.transpose(ps[:, WB1, P // 2 * i:P // 2 * i + P // 2].bitcast(BF16), wm[:, i, :],
                                        ident_bf[:, :])
                last.then_inc(p_wmt, 1)
                shared_down(c, 0)
                pe.wait_ge(v_wmt, at(c, 1, 1))
                weight_rows(c, 0)
                weight_rows(c, 1)
                shared_down(c, 1)
                up(c, 0)
                for e in range(E):
                    if e + 2 < E:
                        weight_rows(c, e + 2)
                    if e + 1 < E:
                        up(c, e + 1)
                    down(c, e)
                    if t is not None and e in SCORE_AT:
                        scores(t, SCORE_AT.index(e) + 2)
                pe.wait_ge(s_add, at(c, E - 1, E - 1))
                for i in range(CT):
                    q = slice(P * i, P * i + P)
                    last = pe.matmul(ps[:, YB, q], yacc[:, q], ident, start=False, stop=(i == CT - 1),
                                     skip_group_check=True)
                last.then_inc(p_y, 1)

            pe.wait_ge(s_ready, 1)
            x_t(0)
            queries(0)
            keys(0)
            values(0)
            for n in range(NSTEP):
                scores(0, n)

            def step(t):
                attend(t - 1)
                x_t(t)
                keys(t)
                o_t(t - 1)
                queries(t)
                attn_out(t - 1)
                values(t)
                scores(t, 0)
                gate(t - 1)
                ffn(t - 1, t)

            step(1)
            with pe.Fori(2, NC) as t:
                step(t)
            attend(NC - 1)
            o_t(NC - 1)
            attn_out(NC - 1)
            gate(NC - 1)
            ffn(NC - 1, None)


N_LOADS = 20 + P // E
SCORE_AT = [1, 3]


def kernel(x, ctx_1024, mask_BxSxS2_bk1, g_xattn, g_ffn, L0_xattn_wq, L0_xattn_bq, L0_xattn_wk, L0_xattn_bk,
           L0_xattn_wv, L0_xattn_bv, L0_xattn_wo, L0_xattn_bo, L0_ffn_gate_w, L0_ffn_w1, L0_ffn_b1, L0_ffn_w2,
           L0_ffn_b2, L0_ffn_w3, L0_ffn_b3, L0_ffn_sw1, L0_ffn_sw2, L0_ffn_sw3):
    import numpy as np
    import concourse.bacc as bacc
    from concourse.bass_utils import run_bass_kernel_spmd as run

    def t(a, *perm):
        return np.ascontiguousarray(np.transpose(np.asarray(a), perm))

    p = np.arange(P)
    consts = np.zeros((P, C_END), np.float32)
    consts[:, C_IDENT:C_IDENT + P] = np.eye(P)
    consts[:, C_IDUP:C_IDUP + S] = p[:, None] % S == np.arange(S)
    consts[:, C_HEADM:C_HEADM + G] = (p[:, None] // DH % G == np.arange(G)) * float(DH) ** -0.5
    consts[:, C_OWN:C_OWN + J] = p[:, None] // S == np.arange(J)
    consts[:, C_IOTA:C_IOTA + E] = np.arange(E)
    consts[:S, C_IDUPQ:C_IDUPQ + P] = p[:S, None] == p % S
    r = np.arange(ROWS)
    sel = (r[:, None] % E == np.arange(E)) & (r[:, None] < 3 * E)
    consts[:ROWS, C_SELW:C_SELW + E * P] = np.repeat(sel, P, axis=1)
    consts[:ROWS, C_PART:C_PART + 3] = r[:, None] // E - 3 == np.arange(3)
    consts[:ROWS, C_ROWE:C_ROWE + E] = (r[:, None] % E == np.arange(E)) & (r[:, None] >= 3 * E)

    arrays = {
        "x": t(np.reshape(x, (NC, CT, P, D)), 0, 2, 1, 3).reshape(NC, P, CT * D),
        "ctxT": t(np.reshape(ctx_1024, (NC, CHUNK, D)), 0, 2, 1),
        "mask": t(np.reshape(mask_BxSxS2_bk1, (NC, CB, S, S)), 0, 2, 1, 3).reshape(NC, S, CB * S),
        "g_x": np.reshape(g_xattn, (1,)), "g_f": np.reshape(g_ffn, (1,)),
        "wqT": t(L0_xattn_wq, 1, 0), "wkT": t(L0_xattn_wk, 1, 0),
        "wvT": t(np.reshape(t(L0_xattn_wv, 1, 0), (D, G, PR, J * DH)), 0, 2, 1, 3).reshape(D, PR, D // 2),
        "woT": t(L0_xattn_wo, 1, 0),
        "bq": np.reshape(L0_xattn_bq, (D, 1)), "bk": np.reshape(L0_xattn_bk, (D, 1)),
        "bv": np.reshape(L0_xattn_bv, (D, 1)), "bo": np.reshape(L0_xattn_bo, (D,)),
        "gateT": t(L0_ffn_gate_w, 1, 0),
        "w1T": t(L0_ffn_w1, 2, 0, 1), "w2T": t(L0_ffn_w2, 2, 0, 1), "w3T": t(L0_ffn_w3, 2, 0, 1),
        "b1T": t(L0_ffn_b1, 1, 0), "b2T": t(L0_ffn_b2, 1, 0), "b3": L0_ffn_b3,
        "sw1T": t(L0_ffn_sw1, 1, 0).reshape(D, SHARED, P), "sw2T": t(L0_ffn_sw2, 1, 0).reshape(D, SHARED, P),
        "sw3T": t(np.reshape(t(L0_ffn_sw3, 1, 0), (SHARED, P, D)), 1, 0, 2),
        "consts": consts,
    }
    nc = bacc.Bacc("TRN2", target_bir_lowering=False, num_devices=1)
    feeds, args = {}, []
    for name, a in arrays.items():
        a = np.ascontiguousarray(a)
        feeds["in_" + name] = a
        args.append(nc.dram_tensor("in_" + name, a.shape, mybir.dt.from_np(a.dtype), kind="ExternalInput").ap())
    args.append(nc.dram_tensor("out_0", (NC, P, CT * D), F32, kind="ExternalOutput").ap())
    build(nc, *args)
    got = run(nc, [feeds], core_ids=[0]).results[0]["out_0"]
    return np.ascontiguousarray(np.transpose(np.reshape(got, (NC, P, CT, D)), (0, 2, 1, 3))).reshape(B, S, D)
```

```python
from contextlib import ExitStack

import concourse.bass as bass
from concourse import mybir

F32 = mybir.dt.float32
F32R = mybir.dt.float32r
BF16 = mybir.dt.bfloat16
U8 = mybir.dt.uint8
U32 = mybir.dt.uint32
ACT = mybir.ActivationFunctionType
ALU = mybir.AluOpType
AX = mybir.AxisListType

B, S, D = 128, 64, 128
HEADS, DH = 16, 8
E = 8
P = 128
CHUNK = 512
NC = B * S // CHUNK
CB = CHUNK // S
CT = CHUNK // P
G, PR, J = 4, 2, 2
VW = DH + 1
SHARED = 2
XS = 3
NEXP = CB // 2
ROWS = 6 * E
EPS = 1e-5
MASKED = -1e20

C_IDENT = 0
C_IDUP = C_IDENT + P
C_HEADM = C_IDUP + S
C_OWN = C_HEADM + G
C_IOTA = C_OWN + J
C_IDUPQ = C_IOTA + E
C_SELW = C_IDUPQ + P
C_PART = C_SELW + E * P
C_ROWE = C_PART + 3
C_END = C_ROWE + E

SC0 = 0
SC1 = 1
PTB = 2
PVB = 3
WBB = 4
G1B, G3B, X2B = 5, 6, 7

ATTEND_AT = {0: [4, 5], 1: [6, 7]}
SCORES_AT = {3: [0, 1], 4: [2, 3], 5: [4, 5], 6: [6, 7]}
DOWN_FIRST = 6


def at(chunk, per_chunk, k):
    return chunk * per_chunk + k


def later(chunk):
    return not (isinstance(chunk, int) and chunk == 0)


def build(nc, x, ctxT, mask, g_x, g_f, wqT, wkT, wvT, woT, bq, bk, bv, bo, gateT, w1T, w2T, w3T,
          b1T, b2T, b3, sw1T, sw2T, sw3T, consts, out):
    with ExitStack() as ctx:
        def sb(name, shape, dt=F32):
            return ctx.enter_context(nc.sbuf_tensor(name, shape, dt))

        def sem(name):
            return ctx.enter_context(nc.semaphore(name))

        cst = sb("cst", [P, C_END])
        ident = cst[:, C_IDENT:C_IDENT + P]
        idup = cst[:, C_IDUP:C_IDUP + S]
        headm = cst[:, C_HEADM:C_HEADM + G]
        own = cst[:, C_OWN:C_OWN + J]
        iota = cst[:, C_IOTA:C_IOTA + E]
        ident_bf = sb("ident_bf", [P, P], BF16)
        idupq_bf = sb("idupq_bf", [S, P], BF16)
        selw = sb("selw", [P, E, P], BF16)
        b3sel = sb("b3sel", [P, E, P], BF16)
        b3row = sb("b3row", [ROWS, P])
        b3part = sb("b3part", [ROWS, 3, P], BF16)
        b3rest = sb("b3rest", [ROWS, P])
        b3pick = sb("b3pick", [ROWS, 2, P])
        wq_s, wk_s = sb("wq_s", [P, D]), sb("wk_s", [P, D])
        wv_s, wo_s = sb("wv_s", [P, PR, D // 2]), sb("wo_s", [P, D])
        gate_s = sb("gate_s", [P, E])
        w1_s, w2_s, w3_s = (sb(n, [P, E, P]) for n in ("w1_s", "w2_s", "w3_s"))
        sw1_s, sw2_s, sw3_s = (sb(n, [P, SHARED, P]) for n in ("sw1_s", "sw2_s", "sw3_s"))
        w1_h, w1_l, w2_h, w2_l, w3_h, w3_l = (
            sb(n, [P, E, P], F32R) for n in ("w1_h", "w1_l", "w2_h", "w2_l", "w3_h", "w3_l"))
        sw1_h, sw1_l, sw2_h, sw2_l = (sb(n, [P, SHARED, P], F32R) for n in ("sw1_h", "sw1_l", "sw2_h", "sw2_l"))
        b1_s, b2_s = sb("b1_s", [P, E]), sb("b2_s", [P, E])
        bq_s, bk_s, bv_s = (sb(n, [P, 1]) for n in ("bq_s", "bk_s", "bv_s"))
        bqm = sb("bqm", [P, G])
        bo_s = sb("bo_s", [P, D])
        gx_s, gf_s = sb("gx_s", [P, 1]), sb("gf_s", [P, 1])
        tgx, tgf = sb("tgx", [P, 1]), sb("tgf", [P, 1])
        pow_s, eps_s = sb("pow_s", [P, CT]), sb("eps_s", [P, CT])

        xin = sb("xin", [P, CT, D])
        cT = sb("cT", [P, CHUNK])
        mk8 = sb("mk8", [S, CB, S], U8)
        mkneg = sb("mkneg", [S, CB, S], BF16)
        bn1, bn2 = sb("bn1", [P, CT, 6]), sb("bn2", [P, CT, 6])
        mv1, mv2 = sb("mv1", [P, CT, 2]), sb("mv2", [P, CT, 2])
        ve1, ve2 = sb("ve1", [P, CT]), sb("ve2", [P, CT])
        rs1, rs2 = sb("rs1", [P, CT]), sb("rs2", [P, CT])
        xn1, xn2 = sb("xn1", [P, CT, D]), sb("xn2", [P, CT, D])
        resid = sb("resid", [P, CT, D])
        xT = sb("xT", [P, CHUNK])
        qexp = sb("qexp", [P, CB, G, S])
        kexp = sb("kexp", [P, G, CHUNK])
        vexp = sb("vexp", [P, CB, G, PR * J * VW])
        smax = sb("smax", [P, 2, PR * G])
        pr = sb("pr", [P, CB, G, PR * S])
        prT = sb("prT", [P, CB, G, P])
        rden = sb("rden", [P, NEXP, 2, HEADS])
        rown = sb("rown", [P, NEXP, 2, HEADS])
        on = sb("on", [P, CB, D])
        oT = sb("oT", [P, CHUNK])
        x1, x1k = sb("x1", [P, CT, D]), sb("x1k", [P, CT, D])
        x2T = sb("x2T", [P, CHUNK])
        lmax, lsum, lrec = sb("lmax", [P, CT]), sb("lsum", [P, CT]), sb("lrec", [P, CT])
        lsub, lexp, score = (sb(n, [P, CT, E]) for n in ("lsub", "lexp", "score"))
        top8 = sb("top8", [P, CT, 8])
        topi = sb("topi", [P, CT, 8], U32)
        topf = sb("topf", [P, CT, 2])
        is0, is1 = sb("is0", [P, CT, E]), sb("is1", [P, CT, E])
        wsel, wr1, wr2 = (sb(n, [P, CT, E]) for n in ("wsel", "wr1", "wr2"))
        wm = sb("wm", [P, CT, P], BF16)
        wmT = sb("wmT", [P, CHUNK], BF16)
        sa = sb("sa", [P, SHARED, CHUNK])
        sh = sb("sh", [P, SHARED, CHUNK])
        xs = sb("xs", [P, XS, CHUNK])
        x2h, x2l = sb("x2h", [P, CHUNK], F32R), sb("x2l", [P, CHUNK], F32R)
        xh, xl = sb("xh", [P, 2, CHUNK], F32R), sb("xl", [P, 2, CHUNK], F32R)
        hb = sb("hb", [P, 2, CHUNK])
        hh, hl = sb("hh", [P, 2, CHUNK], F32R), sb("hl", [P, 2, CHUNK], F32R)
        x3 = sb("x3", [P, 2, CHUNK])
        prod = sb("prod", [P, 4, CHUNK])
        yacc = sb("yacc", [P, CHUNK])
        ob = sb("ob", [P, CT, D])

        ps = ctx.enter_context(nc.psum_tensor("ps", [P, 8, 512], F32))

        s_front, s_back, s_ffn = sem("front_weights_loaded"), sem("back_weights_loaded"), sem("ffn_weights_loaded")
        s_set = sem("setup_step")
        s_ready = sem("setup_ready")
        s_pset = sem("pool_setup")
        s_tanh = sem("tanh_ready")
        s_x, s_ctx, s_mk, s_st = sem("x_loaded"), sem("ctx_loaded"), sem("mask_loaded"), sem("out_stored")
        s_stat1, s_stat2 = sem("ln1_moments"), sem("ln2_moments")
        s_rs2 = sem("ln2_rstd")
        s_pstep, v_step = sem("pool_own_step"), sem("dve_own_step")
        s_rs1, s_xn1, s_res, s_xn2, s_kept, s_add, s_x2l, s_xl, s_hl, s_wlow = (sem(n) for n in (
            "ln1_rstd", "xn1_ready", "resid_ready", "xn2_ready", "x1_kept", "expert_added",
            "x2_low_part", "xs_low_part", "h_low_part", "weights_low_part"))
        p_pt, p_pv, p_ot, p_ao, p_xt, p_q, p_k, p_v = (sem(n) for n in (
            "pe_probsT", "pe_pv", "pe_oT", "pe_attn_out", "pe_xT", "pe_q", "pe_k", "pe_v"))
        p_x2t, p_gate, p_s, p_sa, p_sb, p_wmt = (sem(n) for n in (
            "pe_x2T", "pe_gate", "pe_scores", "pe_shared1", "pe_shared2", "pe_routeT"))
        p_wb, p_g1, p_g3, p_x2, p_y = (sem(n) for n in (
            "pe_weight_rows", "pe_w1", "pe_w3", "pe_w2", "pe_y"))
        a_exp, a_pt, a_ot, a_xt, a_q, a_v, a_x2t, a_ge = (sem(n) for n in (
            "act_probs", "act_probsT", "act_oT", "act_xT", "act_q", "act_v", "act_x2T", "act_gate_exp"))
        a_sa, a_h, a_x3, a_xh, a_whigh, a_mneg = (sem(n) for n in (
            "act_shared", "act_h", "act_x3", "xs_high_part", "weights_high_part", "act_mask"))
        v_pt, v_k, v_max, v_sub, v_rec, v_norm, v_x1 = (sem(n) for n in (
            "dve_probsT", "dve_k", "dve_max", "dve_scores_shifted", "dve_sum_recip",
            "dve_o_normed", "dve_x1"))
        v_lmax, v_lsub, v_wm, v_wmt, v_sh, v_xs, v_prod, v_out = (sem(n) for n in (
            "dve_logit_max", "dve_logits_shifted", "dve_routes", "dve_routeT",
            "dve_shared", "dve_xs", "dve_prod", "dve_out"))

        def bc(ap, axis, n):
            ap = ap.unsqueeze(axis)
            shape = list(ap.shape)
            shape[axis] = n
            return ap.broadcast_to(shape)

        block = ctx.enter_context(nc.Block())

        front_loads = [
            (cst[:, 0:C_SELW], consts[:, 0:C_SELW]), (cst[:, C_PART:C_END], consts[:, C_PART:C_END]),
            (bq_s[:, :], bq), (bk_s[:, :], bk), (wq_s[:, :], wqT), (wk_s[:, :], wkT), (wv_s[:, :, :], wvT)]
        back_loads = [
            (gx_s[:, :], g_x.partition_broadcast(P)), (gf_s[:, :], g_f.partition_broadcast(P)),
            (bo_s[:, :], bo.partition_broadcast(P)), (wo_s[:, :], woT), (bv_s[:, :], bv), (gate_s[:, :], gateT)]
        ffn_loads = [(cst[:, C_SELW:C_PART], consts[:, C_SELW:C_PART])]
        ffn_loads += [(b3row[E * r:E * r + E, :], b3) for r in range(ROWS // E)]
        ffn_loads += [(b1_s[:, :], b1T), (b2_s[:, :], b2T), (sw1_s[:, :, :], sw1T), (sw2_s[:, :, :], sw2T),
                      (w1_s[:, :, :], w1T), (w3_s[:, :, :], w3T), (w2_s[:, :, :], w2T), (sw3_s[:, :, :], sw3T)]
        split_weights = [(sw1_s, sw1_h, sw1_l), (sw2_s, sw2_h, sw2_l), (w1_s, w1_h, w1_l), (w3_s, w3_h, w3_l),
                         (w2_s, w2_h, w2_l)]
        FRONT_LOADED, BACK_LOADED, FFN_LOADED = 16 * len(front_loads), 16 * len(back_loads), 16 * len(ffn_loads)

        @block.sync
        def _(sp):
            def load_x(t):
                if later(t):
                    sp.wait_ge(s_xn1, t)
                    sp.wait_ge(s_res, t)
                sp.dma_start(xin[:, :, :], x[t].rearrange("p (t d) -> p t d", t=CT)).then_inc(s_x, 16)

            def load_ctx(t):
                if later(t):
                    sp.wait_ge(p_v, t)
                    sp.wait_ge(a_mneg, t)
                sp.dma_start(cT[:, :], ctxT[t]).then_inc(s_ctx, 16)
                sp.dma_start(mk8[:, :, :], mask[t].rearrange("q (b k) -> q b k", b=CB)).then_inc(s_mk, 16)

            def store(c):
                sp.wait_ge(v_out, at(c, 1, 1))
                sp.dma_start(out[c].rearrange("p (t d) -> p t d", t=CT), ob[:, :, :]).then_inc(s_st, 16)

            load_x(0)
            load_ctx(0)
            for dst, src in back_loads:
                sp.dma_start(dst, src).then_inc(s_back, 16)
            for m in (1, 2, 3):
                load_ctx(m)
                load_x(m)
            with sp.Fori(0, NC - 4) as c:
                m = sp.snap(c + 4)
                store(c)
                load_ctx(m)
                load_x(m)
            for c in range(NC - 4, NC):
                store(c)
            sp.wait_ge(s_st, 16 * NC)

        @block.gpsimd
        def _(pool):
            pool.memset(pow_s[:, :], -0.5).then_inc(s_pset, 1)
            pool.memset(eps_s[:, :], EPS).then_inc(s_pset, 1)
            pool.wait_ge(s_pset, 2)

            def rstd(stat, k, ve, rs, mv):
                pool.wait_ge(stat, at(k, 1, 1))
                pool.tensor_tensor(ve[:, :], mv[:, :, 1], eps_s[:, :], ALU.add).then_inc(s_pstep, 1)
                pool.wait_ge(s_pstep, 1)
                return pool.tensor_tensor(rs[:, :], ve[:, :], pow_s[:, :], ALU.pow)

            def front(m):
                pool.sem_clear(s_pstep)
                if later(m):
                    pool.wait_ge(s_xn1, m)
                rstd(s_stat1, m, ve1, rs1, mv1).then_inc(s_rs1, 1)

            def keep(m):
                if later(m):
                    pool.wait_ge(v_x1, m)
                pool.tensor_tensor(resid[:, :, :], xin[:, :, :], bc(bo_s[:, :], 1, CT), ALU.add).then_inc(s_res, 1)

            def back(n):
                pool.sem_clear(s_pstep)
                if later(n):
                    pool.wait_ge(s_xn2, n)
                rstd(s_stat2, n, ve2, rs2, mv2).then_inc(s_rs2, 1)

            def x2_low(n):
                pool.wait_ge(a_x2t, at(n, 1, 1))
                pool.tensor_tensor(x2l[:, :], x2T[:, :], x2h[:, :].bitcast(F32), ALU.subtract).then_inc(s_x2l, 1)

            def x_low(c, e):
                pool.wait_ge(a_xh, at(c, E, e + 1))
                pool.tensor_tensor(xl[:, e % 2, :], xs[:, e % XS, :], xh[:, e % 2, :].bitcast(F32),
                                   ALU.subtract).then_inc(s_xl, 1)

            def h_low(c, e):
                pool.wait_ge(a_h, at(c, E, e + 1))
                pool.tensor_tensor(hl[:, e % 2, :], hb[:, e % 2, :], hh[:, e % 2, :].bitcast(F32),
                                   ALU.subtract).then_inc(s_hl, 1)

            def add_expert(c, e):
                pool.wait_ge(v_prod, at(c, E, e + 1))
                if e == 1:
                    if later(c):
                        pool.wait_ge(p_y, c)
                    first = prod[:, 0, :]
                else:
                    pool.wait_ge(s_add, at(c, E - 1, e - 1))
                    first = yacc[:, :]
                pool.tensor_tensor(yacc[:, :], first, prod[:, e % 4, :], ALU.add).then_inc(s_add, 1)

            def step(c, n, m):
                if c is not None:
                    x_low(c, 0)
                    x_low(c, 1)
                    h_low(c, 0)
                for e in range(E):
                    if e == 6 and n is not None:
                        x2_low(n)
                    if c is not None and e + 2 < E:
                        x_low(c, e + 2)
                    if c is not None and e + 1 < E:
                        h_low(c, e + 1)
                    if e == 0 and m is not None:
                        front(m)
                    if e == 3 and n is not None:
                        back(n)
                    if c is not None and e >= 1:
                        add_expert(c, e)
                    if e == 6 and m is not None:
                        keep(m)

            front(0)
            pool.memset(kexp[:, :, :], 0.0).then_inc(s_pset, 1)
            pool.memset(vexp[:, :, :, :], 0.0).then_inc(s_pset, 1)
            pool.memset(wm[:, :, :], 0.0).then_inc(s_pset, 1)
            pool.memset(b3sel[:, :, :], 0.0).then_inc(s_pset, 1)
            pool.wait_ge(s_pset, 6)
            for pair in range(PR):
                ones = vexp[S * pair:S * pair + S, :, :, :].rearrange("q b g (p j n) -> q (b g) p j n", p=PR, j=J)
                pool.memset(ones[:, :, pair, :, DH], 1.0).then_inc(s_pset, 1)
            pool.wait_ge(s_ready, 2)
            keep(0)
            step(None, 0, 1)
            for k, (whole, high, low) in enumerate(split_weights):
                pool.wait_ge(a_whigh, k + 1)
                pool.tensor_tensor(low[:, :, :], whole[:, :, :], high[:, :, :].bitcast(F32), ALU.subtract).then_inc(s_wlow, 1)
            step(0, 1, 2)
            with pool.Fori(1, NC - 2) as c:
                step(c, c + 1, c + 2)
            step(NC - 2, NC - 1, None)
            step(NC - 1, None, None)

        @block.scalar
        def _(act):
            for dst, src in front_loads:
                act.dma_start(dst, src).then_inc(s_front, 16)
            for dst, src in ffn_loads:
                act.dma_start(dst, src).then_inc(s_ffn, 16)

            def probs(m):
                for i in range(NEXP):
                    act.wait_ge(v_sub, at(m, CB, 2 * i + 2))
                    p2 = pr[:, 2 * i:2 * i + 2, :, :].rearrange("q b g k -> q (b g k)")
                    act.activation(p2, p2, ACT.Exp).then_inc(a_exp, 1)

            def probs_t(n, b):
                act.wait_ge(p_pt, at(n, CB, b + 1))
                if later(n):
                    act.wait_ge(p_pv, at(n, NEXP, 0))
                act.activation(prT[:, b, :, :].rearrange("p g q -> p (g q)"), ps[:, PTB, :], ACT.Copy).then_inc(a_pt, 1)

            def o_t(n):
                act.wait_ge(p_ot, at(n, 1, 1))
                if later(n):
                    act.wait_ge(p_ao, n)
                act.activation(oT[:, :], ps[:, PVB, :], ACT.Identity, bias=bv_s[:, :]).then_inc(a_ot, 1)

            def x_t(m):
                act.wait_ge(p_xt, at(m, 1, 1))
                if later(m):
                    act.wait_ge(p_q, m)
                act.activation(xT[:, :], ps[:, PTB, :], ACT.Copy).then_inc(a_xt, 1)

            def queries(m):
                act.wait_ge(p_q, at(m, 1, 1))
                if later(m):
                    act.wait_ge(p_s, at(m, CB, 0))
                for k in range(G):
                    last = act.activation(qexp[:, :, k, :], ps[:, SC1, :].rearrange("p (b q) -> p b q", q=S),
                                          ACT.Identity, bias=bqm[:, k:k + 1], scale=headm[:, k:k + 1])
                last.then_inc(a_q, 1)

            def values(m):
                act.wait_ge(p_v, at(m, 1, 1))
                if later(m):
                    act.wait_ge(p_pv, at(m, NEXP, 0))
                for pair in range(PR):
                    q = slice(S * pair, S * pair + S)
                    dst = vexp[q, :, :, :].rearrange("q b g (p j n) -> q (b g) p j n", p=PR, j=J)
                    last = act.activation(dst[:, :, pair, :, 0:DH],
                                          ps[q, PTB, :].rearrange("q (a j n) -> q a j n", j=J, n=DH), ACT.Copy)
                last.then_inc(a_v, 1)

            def x2_t(n):
                act.wait_ge(p_x2t, at(n, 1, 1))
                if later(n):
                    act.wait_ge(p_gate, n)
                    act.wait_ge(p_sb, at(n, SHARED, 0))
                    act.wait_ge(v_xs, at(n, E, 0))
                act.activation(x2T[:, :], ps[:, PTB, :], ACT.Copy)
                act.activation(x2h[:, :], ps[:, PTB, :], ACT.Copy).then_inc(a_x2t, 1)

            def gate_exp(n):
                act.wait_ge(v_lsub, at(n, 1, 1))
                act.activation(lexp[:, :, :], lsub[:, :, :], ACT.Exp).then_inc(a_ge, 1)

            def mask_bias(m):
                act.wait_ge(s_mk, at(m, 16, 16))
                if later(m):
                    act.wait_ge(p_s, at(m, CB, 0))
                act.activation(mkneg[:, :, :], mk8[:, :, :], ACT.Copy, scale=MASKED).then_inc(a_mneg, 1)

            def keep_x1(c):
                act.wait_ge(v_x1, at(c, 1, 1))
                if later(c):
                    act.wait_ge(v_out, c)
                act.activation(x1k[:, :, :], x1[:, :, :], ACT.Copy).then_inc(s_kept, 1)

            def shared(c, k):
                act.wait_ge(p_sa, at(c, SHARED, k + 1))
                if later(c):
                    act.wait_ge(v_sh, at(c, SHARED, 0))
                act.activation(sa[:, k, :], ps[:, G1B, :], ACT.Silu).then_inc(a_sa, 1)

            def x_high(c, e):
                act.wait_ge(v_xs, at(c, E, e + 1))
                if e >= 2:
                    act.wait_ge(p_g3, at(c, E, e - 1))
                act.activation(xh[:, e % 2, :], xs[:, e % XS, :], ACT.Copy).then_inc(a_xh, 1)

            def expert(c, e):
                act.wait_ge(p_g1, at(c, E, e + 1))
                if e >= 2:
                    act.wait_ge(p_x2, at(c, E, e - 1))
                act.activation(hb[:, e % 2, :], ps[:, G1B, :], ACT.Silu, bias=b1_s[:, e:e + 1])
                act.activation(hh[:, e % 2, :], ps[:, G1B, :], ACT.Silu, bias=b1_s[:, e:e + 1]).then_inc(a_h, 1)
                act.wait_ge(p_g3, at(c, E, e + 1))
                if e >= 2:
                    act.wait_ge(v_prod, at(c, E, e - 1))
                act.activation(x3[:, e % 2, :], ps[:, G3B, :], ACT.Copy).then_inc(a_x3, 1)

            def step(c, n, m):
                if c is not None:
                    shared(c, 0)
                if n is not None:
                    probs_t(n, 0)
                if c is not None:
                    shared(c, 1)
                if n is not None:
                    probs_t(n, 2)
                if c is not None:
                    x_high(c, 0)
                    x_high(c, 1)
                    expert(c, 0)
                for e in range(E):
                    if c is not None and e + 2 < E:
                        x_high(c, e + 2)
                    if n is not None and e in ATTEND_AT:
                        probs_t(n, ATTEND_AT[e][0])
                    if c is not None and e + 1 < E:
                        expert(c, e + 1)
                    if e == 0 and c is not None:
                        keep_x1(c)
                    if e == 0 and m is not None:
                        mask_bias(m)
                    if e == 1 and m is not None:
                        x_t(m)
                    if e == 2 and n is not None:
                        o_t(n)
                    if e == 2 and m is not None:
                        queries(m)
                    if e == 3 and m is not None:
                        values(m)
                    if e == 5 and n is not None:
                        x2_t(n)
                if n is not None:
                    gate_exp(n)
                if m is not None:
                    probs(m)

            act.wait_ge(s_ready, 1)
            x_t(0)
            queries(0)
            mask_bias(0)
            act.wait_ge(s_pset, 8)
            values(0)
            act.wait_ge(s_back, BACK_LOADED)
            act.activation(tgx[:, :], gx_s[:, :], ACT.Tanh).then_inc(s_tanh, 1)
            act.activation(tgf[:, :], gf_s[:, :], ACT.Tanh).then_inc(s_tanh, 1)
            probs(0)
            act.wait_ge(s_ffn, FFN_LOADED)
            for whole, high, low in split_weights:
                act.activation(high[:, :, :], whole[:, :, :], ACT.Copy).then_inc(a_whigh, 1)
            step(None, 0, 1)
            step(0, 1, 2)
            with act.Fori(1, NC - 2) as c:
                step(c, c + 1, c + 2)
            step(NC - 2, NC - 1, None)
            step(NC - 1, None, None)

        @block.vector
        def _(dve):
            setup_steps = [0]

            def setup_link(ins):
                setup_steps[0] += 1
                ins.then_inc(s_set, 1)
                dve.wait_ge(s_set, setup_steps[0])

            def setup_front():
                dve.wait_ge(s_front, FRONT_LOADED)
                dve.tensor_scalar(bqm[:, :], headm, bq_s[:, 0:1], None, ALU.mult)
                dve.tensor_copy(idupq_bf[:, :], cst[0:S, C_IDUPQ:C_IDUPQ + P]).then_inc(s_ready, 1)

            def setup_back():
                dve.wait_ge(s_back, BACK_LOADED)
                dve.wait_ge(s_tanh, 2)
                dve.tensor_scalar(wo_s[:, :], wo_s[:, :], tgx[:, 0:1], None, ALU.mult)
                dve.tensor_scalar(bo_s[:, :], bo_s[:, :], tgx[:, 0:1], None, ALU.mult).then_inc(s_ready, 1)

            def setup_ffn():
                dve.wait_ge(s_ffn, FFN_LOADED)
                dve.tensor_copy(ident_bf[:, :], ident)
                dve.tensor_copy(selw[:, :, :].rearrange("r e p -> r (e p)"), cst[:, C_SELW:C_SELW + E * P])
                setup_link(dve.tensor_copy(b3part[:, 0, :], b3row[:, :]))
                setup_link(dve.tensor_tensor(b3rest[:, :], b3row[:, :], b3part[:, 0, :], ALU.subtract))
                setup_link(dve.tensor_copy(b3part[:, 1, :], b3rest[:, :]))
                setup_link(dve.tensor_tensor(b3part[:, 2, :], b3rest[:, :], b3part[:, 1, :], ALU.subtract))
                part = [cst[0:ROWS, C_PART + k:C_PART + k + 1] for k in range(3)]
                setup_link(dve.tensor_scalar(b3pick[:, 0, :], b3part[:, 0, :], part[0], None, ALU.mult))
                setup_link(dve.scalar_tensor_tensor(b3pick[:, 1, :], b3part[:, 1, :], part[1], b3pick[:, 0, :],
                                                    ALU.mult, ALU.add))
                setup_link(dve.scalar_tensor_tensor(b3pick[:, 0, :], b3part[:, 2, :], part[2], b3pick[:, 1, :],
                                                    ALU.mult, ALU.add))
                for e in range(E):
                    last = dve.tensor_scalar(b3sel[0:ROWS, e, :], b3pick[:, 0, :],
                                             cst[0:ROWS, C_ROWE + e:C_ROWE + e + 1], None, ALU.mult)
                last.then_inc(s_ready, 1)

            def stats(src, bn, mv, done):
                for i in range(CT):
                    last = dve.bn_stats(bn[:, i, :], src[:, i, :])
                last.then_inc(v_step, 1)
                dve.wait_ge(v_step, 1)
                for i in range(CT):
                    last = dve.bn_aggr(mv[:, i, :], bn[:, i, :])
                last.then_inc(done, 1)

            def front_stats(m):
                dve.sem_clear(v_step)
                dve.wait_ge(s_x, at(m, 16, 16))
                if later(m):
                    dve.wait_ge(s_rs1, m)
                stats(xin, bn1, mv1, s_stat1)

            def ln1(m):
                dve.wait_ge(s_rs1, at(m, 1, 1))
                if later(m):
                    dve.wait_ge(p_xt, m)
                for i in range(CT):
                    last = dve.tensor_scalar(xn1[:, i, :], xin[:, i, :], mv1[:, i, 0:1], rs1[:, i:i + 1],
                                             ALU.subtract, ALU.mult)
                last.then_inc(s_xn1, 1)

            def probs_t(n, b):
                dve.wait_ge(p_pt, at(n, CB, b + 1))
                if later(n):
                    dve.wait_ge(p_pv, at(n, NEXP, 0))
                dve.tensor_copy(prT[:, b, :, :].rearrange("p g q -> p (g q)"), ps[:, PTB, :]).then_inc(v_pt, 1)

            def norm(n, i):
                dve.wait_ge(p_pv, at(n, NEXP, i + 1))
                o = ps[:, SC1 if i % 2 else PVB, :].rearrange("q (s w) -> q s w", s=2)[:, :, 0:HEADS * VW].rearrange(
                    "q b (h n) -> q b h n", n=VW)
                dve.reciprocal(rden[:, i, :, :], o[:, :, :, DH]).then_inc(v_rec, 1)
                dve.wait_ge(v_rec, at(n, 2 * NEXP, 2 * i + 1))
                dve.tensor_tensor(rown[:, i, :, :].rearrange("q b (a j) -> q (b a) j", j=J),
                                  rden[:, i, :, :].rearrange("q b (a j) -> q (b a) j", j=J),
                                  bc(own, 1, 2 * HEADS // J), ALU.mult).then_inc(v_rec, 1)
                dve.wait_ge(v_rec, at(n, 2 * NEXP, 2 * i + 2))
                if later(n):
                    dve.wait_ge(p_ot, n)
                dve.tensor_tensor(on[:, 2 * i:2 * i + 2, :].rearrange("q b (h d) -> q b h d", d=DH),
                                  o[:, :, :, 0:DH], bc(rown[:, i, :, :], 3, DH), ALU.mult).then_inc(v_norm, 1)

            def residual(n):
                dve.sem_clear(v_step)
                dve.wait_ge(p_ao, at(n, 1, 1))
                dve.wait_ge(s_res, at(n, 1, 1))
                if later(n):
                    dve.wait_ge(s_kept, n)
                dve.tensor_tensor(x1[:, :, :], ps[:, PVB, :].rearrange("q (t d) -> q t d", t=CT), resid[:, :, :],
                                  ALU.add).then_inc(v_x1, 1)
                dve.wait_ge(v_x1, at(n, 1, 1))
                stats(x1, bn2, mv2, s_stat2)

            def ln2(n):
                dve.wait_ge(s_rs2, at(n, 1, 1))
                if later(n):
                    dve.wait_ge(p_x2t, n)
                for i in range(CT):
                    last = dve.tensor_scalar(xn2[:, i, :], x1[:, i, :], mv2[:, i, 0:1], rs2[:, i:i + 1],
                                             ALU.subtract, ALU.mult)
                last.then_inc(s_xn2, 1)

            def keys(m):
                dve.wait_ge(p_k, at(m, 1, 1))
                if later(m):
                    dve.wait_ge(p_s, at(m, CB, 0))
                for g in range(G):
                    q = slice(32 * g, 32 * g + 32)
                    last = dve.tensor_scalar(kexp[q, g, :], ps[q, SC0, :], bk_s[q, 0:1], None, ALU.add)
                last.then_inc(v_k, 1)

            def gate_max(n):
                logit = ps[:, PVB, 0:CT * E].rearrange("q (t e) -> q t e", e=E)
                dve.wait_ge(p_gate, at(n, 1, 1))
                dve.reduce_max(lmax[:, :], logit, AX.X).then_inc(v_lmax, 1)
                dve.wait_ge(v_lmax, at(n, 1, 1))
                dve.tensor_tensor(lsub[:, :, :], logit, bc(lmax[:, :], 2, E), ALU.subtract).then_inc(v_lsub, 1)

            def route(c):
                n = [0]

                def link(ins):
                    n[0] += 1
                    ins.then_inc(v_step, 1)
                    dve.wait_ge(v_step, n[0])

                dve.sem_clear(v_step)
                dve.wait_ge(a_ge, at(c, 1, 1))
                link(dve.reduce_sum(lsum[:, :], lexp[:, :, :], AX.X))
                link(dve.reciprocal(lrec[:, :], lsum[:, :]))
                link(dve.tensor_tensor(score[:, :, :], lexp[:, :, :], bc(lrec[:, :], 2, E), ALU.mult))
                for i in range(CT):
                    last = dve.max(top8[:, i, :], score[:, i, :])
                link(last)
                for i in range(CT):
                    last = dve.max_index(topi[:, i, :], top8[:, i, :], score[:, i, :])
                link(last)
                link(dve.tensor_copy(topf[:, :, :], topi[:, :, 0:2]))
                dve.tensor_tensor(is0[:, :, :], bc(iota, 1, CT), bc(topf[:, :, 0], 2, E), ALU.is_equal)
                link(dve.tensor_tensor(is1[:, :, :], bc(iota, 1, CT), bc(topf[:, :, 1], 2, E), ALU.is_equal))
                if later(c):
                    dve.wait_ge(p_wmt, c)
                link(dve.tensor_tensor(is1[:, :, :], is0[:, :, :], is1[:, :, :], ALU.add))
                dve.tensor_copy(wm[:, :, 3 * E:ROWS].rearrange("q t (r e) -> q t r e", r=3), bc(is1[:, :, :], 2, 3))
                link(dve.tensor_tensor(wsel[:, :, :], score[:, :, :], is1[:, :, :], ALU.mult))
                link(dve.tensor_copy(wm[:, :, 0:E], wsel[:, :, :]))
                link(dve.tensor_tensor(wr1[:, :, :], wsel[:, :, :], wm[:, :, 0:E], ALU.subtract))
                link(dve.tensor_copy(wm[:, :, E:2 * E], wr1[:, :, :]))
                dve.tensor_tensor(wm[:, :, 2 * E:3 * E], wr1[:, :, :], wm[:, :, E:2 * E],
                                  ALU.subtract).then_inc(v_wm, 1)

            def scores(m, b):
                s4 = ps[:, SC1 if b % 2 else SC0, :].rearrange("q (a k) -> q a k", k=S)
                dve.wait_ge(p_s, at(m, CB, b + 1))
                dve.reduce_max(smax[:, b % 2, :], s4, AX.X).then_inc(v_max, 1)
                dve.wait_ge(v_max, at(m, CB, b + 1))
                if later(m):
                    dve.wait_ge(p_pt, at(m, CB, 0))
                dve.tensor_tensor(pr[:, b, :, :].rearrange("q g (p k) -> q (g p) k", k=S), s4,
                                  bc(smax[:, b % 2, :], 2, S), ALU.subtract).then_inc(v_sub, 1)

            def shared(c, k):
                dve.wait_ge(a_sa, at(c, SHARED, k + 1))
                dve.wait_ge(p_sb, at(c, SHARED, k + 1))
                if later(c):
                    dve.wait_ge(p_y, c)
                dve.tensor_tensor(sh[:, k, :], ps[:, G3B, :], sa[:, k, :], ALU.mult).then_inc(v_sh, 1)

            def routes_t(c):
                dve.wait_ge(p_wmt, at(c, 1, 1))
                if later(c):
                    dve.wait_ge(p_g3, at(c, E, 0))
                dve.tensor_copy(wmT[:, :], ps[:, WBB, 0:CHUNK // 2].bitcast(BF16)).then_inc(v_wmt, 1)

            def scale_x(c, e):
                dve.wait_ge(p_wb, at(c, E, e + 1))
                if e >= XS:
                    dve.wait_ge(s_xl, at(c, E, e - XS + 1))
                dve.tensor_tensor(xs[:, e % XS, :], ps[:, WBB, :], x2T[:, :], ALU.mult).then_inc(v_xs, 1)

            def combine(c, e):
                dve.wait_ge(p_x2, at(c, E, e + 1))
                dve.wait_ge(a_x3, at(c, E, e + 1))
                if e >= 4:
                    dve.wait_ge(s_add, at(c, E - 1, max(e - 4, 1)))
                elif later(c):
                    dve.wait_ge(s_add, at(c, E - 1, 0))
                dve.scalar_tensor_tensor(prod[:, e % 4, :], ps[:, X2B, :], b2_s[:, e:e + 1], x3[:, e % 2, :],
                                         ALU.add, ALU.mult).then_inc(v_prod, 1)

            def output(c):
                dve.wait_ge(p_y, at(c, 1, 1))
                dve.wait_ge(s_kept, at(c, 1, 1))
                if later(c):
                    dve.wait_ge(s_st, at(c, 16, 0))
                dve.scalar_tensor_tensor(ob[:, :, :].rearrange("q t d -> q (t d)"), ps[:, SC0, :], tgf[:, 0:1],
                                         x1k[:, :, :].rearrange("q t d -> q (t d)"), ALU.mult, ALU.add).then_inc(v_out, 1)

            def step(c, n, m):
                if c is not None:
                    route(c)
                    if later(c):
                        output(c - 1)
                if c is not None:
                    shared(c, 0)
                    routes_t(c)
                if n is not None:
                    probs_t(n, 1)
                if c is not None:
                    shared(c, 1)
                if c is not None:
                    scale_x(c, 0)
                    scale_x(c, 1)
                if n is not None:
                    norm(n, 0)
                    probs_t(n, 3)
                for e in range(E):
                    if c is not None and e + 2 < E:
                        scale_x(c, e + 2)
                    if e == 0 and m is not None:
                        front_stats(m)
                    if n is not None and e in ATTEND_AT:
                        norm(n, ATTEND_AT[e][0] // 2 - 1)
                        probs_t(n, ATTEND_AT[e][1])
                    if e == 1 and m is not None:
                        ln1(m)
                    if e == 1 and n is not None:
                        norm(n, NEXP - 1)
                    if e == 2 and m is not None:
                        keys(m)
                    if e == 3 and n is not None:
                        residual(n)
                    if c is not None and e >= DOWN_FIRST:
                        combine(c, e)
                    if e == 6 and n is not None:
                        gate_max(n)
                    if e == 4 and n is not None:
                        ln2(n)
                    if m is not None:
                        for b in SCORES_AT.get(e, []):
                            scores(m, b)
                    if c is not None and e < DOWN_FIRST:
                        combine(c, e)

            front_stats(0)
            setup_front()
            ln1(0)
            dve.wait_ge(s_pset, 8)
            keys(0)
            setup_back()
            for b in range(CB):
                scores(0, b)
            step(None, 0, 1)
            setup_ffn()
            step(0, 1, 2)
            with dve.Fori(1, NC - 2) as c:
                step(c, c + 1, c + 2)
            step(NC - 2, NC - 1, None)
            step(NC - 1, None, None)
            output(NC - 1)

        @block.tensor
        def _(pe):
            def product(bank, w_high, w_low, x_high, x_low, start):
                pe.matmul(ps[:, bank, :], w_low, x_high, start=start, stop=False)
                pe.matmul(ps[:, bank, :], w_high, x_low, start=False, stop=False)
                return pe.matmul(ps[:, bank, :], w_high, x_high, start=False, stop=True)

            def probs_t(n, c, b):
                if b % 2 == 0:
                    pe.wait_ge(a_exp, at(n, NEXP, b // 2 + 1))
                if b == 0:
                    pe.wait_ge(a_v, at(n, 1, 1))
                    if c is not None:
                        pe.wait_ge(a_x2t, at(c, 1, 1))
                elif b % 2:
                    pe.wait_ge(a_pt, at(n, NEXP, b // 2 + 1))
                else:
                    pe.wait_ge(v_pt, at(n, NEXP, b // 2))
                for g in range(G):
                    last = pe.transpose(ps[:, PTB, g * P:g * P + P], pr[:, b, g, :], ident)
                last.then_inc(p_pt, 1)

            def pv(n, c, b):
                if b == 0 and c is not None:
                    pe.wait_ge(v_lsub, at(c, 1, 1))
                if b == 2:
                    pe.wait_ge(v_sub, at(n, CB, CB))
                if b % 2 == 0 and b >= 4:
                    pe.wait_ge(v_norm, at(n, NEXP, b // 2 - 1))
                if b % 2:
                    pe.wait_ge(v_pt, at(n, NEXP, b // 2 + 1))
                else:
                    pe.wait_ge(a_pt, at(n, NEXP, b // 2 + 1))
                bank = SC1 if b // 2 % 2 else PVB
                w = PR * J * VW
                for g in range(G):
                    last = pe.matmul(ps[:, bank, 256 * (b % 2) + w * g:256 * (b % 2) + w * g + w],
                                     prT[:, b, g, :], vexp[:, b, g, :], start=True, stop=True)
                if b % 2:
                    last.then_inc(p_pv, 1)

            def attend(n, c, b):
                if b < CB:
                    probs_t(n, c, b)
                if b:
                    pv(n, c, b - 1)

            def o_t(n):
                pe.wait_ge(v_norm, at(n, NEXP, NEXP))
                for b in range(CB):
                    last = pe.matmul(ps[:, PVB, S * b:S * b + S], on[:, b, :], idup, start=True, stop=True)
                last.then_inc(p_ot, 1)

            def attn_out(n):
                pe.wait_ge(a_ot, at(n, 1, 1))
                for i in range(CT):
                    last = pe.matmul(ps[:, PVB, P * i:P * i + P], oT[:, P * i:P * i + P], wo_s[:, :],
                                     start=True, stop=True)
                last.then_inc(p_ao, 1)

            def x_t(m, n):
                pe.wait_ge(s_xn1, at(m, 1, 1))
                if n is not None:
                    pe.wait_ge(v_pt, at(n, NEXP, NEXP))
                for i in range(CT):
                    last = pe.transpose(ps[:, PTB, P * i:P * i + P], xn1[:, i, :], ident)
                last.then_inc(p_xt, 1)

            def queries(m, n):
                pe.wait_ge(a_xt, at(m, 1, 1))
                if n is not None:
                    pe.wait_ge(v_norm, at(n, NEXP, NEXP))
                pe.matmul(ps[:, SC1, :], wq_s[:, :], xT[:, :], start=True, stop=True).then_inc(p_q, 1)

            def keys(m, n, c):
                pe.wait_ge(s_ctx, at(m, 16, 16))
                if c is not None and later(c):
                    pe.wait_ge(v_out, c)
                elif n is not None:
                    pe.wait_ge(v_sub, at(n, CB, CB))
                pe.matmul(ps[:, SC0, :], wk_s[:, :], cT[:, :], start=True, stop=True).then_inc(p_k, 1)

            def values(m):
                pe.wait_ge(a_xt, at(m, 1, 1))
                for b in range(CB):
                    for pair in range(PR):
                        last = pe.matmul(ps[S * pair:S * pair + S, PTB, S * b:S * b + S], cT[:, S * b:S * b + S],
                                         wv_s[:, pair, :], start=True, stop=True)
                last.then_inc(p_v, 1)

            def scores(m, b):
                if b == 0:
                    pe.wait_ge(a_q, at(m, 1, 1))
                    pe.wait_ge(v_k, at(m, 1, 1))
                    pe.wait_ge(a_mneg, at(m, 1, 1))
                if b >= 2:
                    pe.wait_ge(v_sub, at(m, CB, b - 1))
                bank = SC1 if b % 2 else SC0
                pe.matmul(ps[:, bank, :].rearrange("q (a k) -> q a k", k=S), idupq_bf[:, :],
                          bc(mkneg[:, b, :], 1, PR * G), start=True, stop=False)
                for pair in range(PR):
                    last = pe.matmul(ps[:, bank, :].rearrange("q (g p k) -> q g p k", g=G, p=PR)[:, :, pair, :],
                                     qexp[:, b, 2 * pair:2 * pair + 2, :].rearrange("f m q -> f (m q)"),
                                     kexp[:, :, S * b:S * b + S], start=False, stop=(pair == PR - 1))
                last.then_inc(p_s, 1)

            def x2_t(n, m):
                pe.wait_ge(s_xn2, at(n, 1, 1))
                if m is not None:
                    pe.wait_ge(a_v, at(m, 1, 1))
                else:
                    pe.wait_ge(v_pt, at(n, NEXP, NEXP))
                for i in range(CT):
                    last = pe.transpose(ps[:, PTB, P * i:P * i + P], xn2[:, i, :], ident)
                last.then_inc(p_x2t, 1)

            def gate(n):
                pe.wait_ge(a_x2t, at(n, 1, 1))
                pe.wait_ge(v_x1, at(n, 1, 1))
                for i in range(CT):
                    last = pe.matmul(ps[:, PVB, E * i:E * i + E], x2T[:, P * i:P * i + P], gate_s[:, :],
                                     start=True, stop=True)
                last.then_inc(p_gate, 1)

            def shared(c, k):
                if k:
                    pe.wait_ge(a_sa, at(c, SHARED, k))
                elif later(c):
                    pe.wait_ge(a_h, at(c, E, 0))
                if not k:
                    pe.wait_ge(s_x2l, at(c, 1, 1))
                product(G1B, sw1_h[:, k, :], sw1_l[:, k, :], x2h[:, :], x2l[:, :], True).then_inc(p_sa, 1)
                if k:
                    pe.wait_ge(v_sh, at(c, SHARED, k))
                elif later(c):
                    pe.wait_ge(a_x3, at(c, E, 0))
                product(G3B, sw2_h[:, k, :], sw2_l[:, k, :], x2h[:, :], x2l[:, :], True).then_inc(p_sb, 1)

            def routes_t(c):
                pe.wait_ge(v_wm, at(c, 1, 1))
                if later(c):
                    pe.wait_ge(v_xs, at(c, E, 0))
                for i in range(CT):
                    last = pe.transpose(ps[:, WBB, P // 2 * i:P // 2 * i + P // 2].bitcast(BF16), wm[:, i, :],
                                        ident_bf[:, :])
                last.then_inc(p_wmt, 1)

            def weight_rows(c, e):
                if e:
                    pe.wait_ge(v_xs, at(c, E, e))
                else:
                    pe.wait_ge(v_wmt, at(c, 1, 1))
                pe.matmul(ps[:, WBB, :], selw[:, e, :], wmT[:, :], start=True, stop=True).then_inc(p_wb, 1)

            def up(c, e):
                pe.wait_ge(s_xl, at(c, E, e + 1))
                if e:
                    pe.wait_ge(a_h, at(c, E, e))
                else:
                    pe.wait_ge(a_sa, at(c, SHARED, SHARED))
                product(G1B, w1_h[:, e, :], w1_l[:, e, :], xh[:, e % 2, :], xl[:, e % 2, :], True).then_inc(p_g1, 1)
                if e:
                    pe.wait_ge(a_x3, at(c, E, e))
                else:
                    pe.wait_ge(v_sh, at(c, SHARED, SHARED))
                pe.matmul(ps[:, G3B, :], b3sel[:, e, :], wmT[:, :], start=True, stop=False)
                product(G3B, w3_h[:, e, :], w3_l[:, e, :], xh[:, e % 2, :], xl[:, e % 2, :], False).then_inc(p_g3, 1)

            def down(c, e):
                pe.wait_ge(s_hl, at(c, E, e + 1))
                if e:
                    pe.wait_ge(v_prod, at(c, E, e))
                elif later(c):
                    pe.wait_ge(v_prod, at(c, E, 0))
                product(X2B, w2_h[:, e, :], w2_l[:, e, :], hh[:, e % 2, :], hl[:, e % 2, :], True).then_inc(p_x2, 1)

            def shared_down(c, m):
                pe.wait_ge(v_sh, at(c, SHARED, SHARED))
                if m is not None:
                    pe.wait_ge(v_sub, at(m, CB, CB))
                else:
                    pe.wait_ge(v_out, c)
                for k in range(SHARED):
                    for i in range(CT):
                        q = slice(P * i, P * i + P)
                        pe.matmul(ps[:, SC0, q], sh[:, k, q], sw3_s[:, k, :], start=(k == 0 and i == 0), stop=False,
                                  skip_group_check=True)

            def experts_sum(c):
                pe.wait_ge(s_add, at(c, E - 1, E - 1))
                for i in range(CT):
                    q = slice(P * i, P * i + P)
                    last = pe.matmul(ps[:, SC0, q], yacc[:, q], ident, start=False, stop=(i == CT - 1),
                                     skip_group_check=True)
                last.then_inc(p_y, 1)

            def step(c, n, m):
                if c is not None:
                    shared(c, 0)
                    if later(c):
                        shared_down(c - 1, n)
                if n is not None:
                    attend(n, c, 0)
                if c is not None:
                    if later(c):
                        experts_sum(c - 1)
                    routes_t(c)
                if n is not None:
                    attend(n, c, 1)
                if c is not None:
                    shared(c, 1)
                    weight_rows(c, 0)
                if n is not None:
                    attend(n, c, 2)
                if c is not None:
                    weight_rows(c, 1)
                if n is not None:
                    attend(n, c, 3)
                if c is not None:
                    up(c, 0)
                for e in range(E):
                    if c is not None and e + 2 < E:
                        weight_rows(c, e + 2)
                    if n is not None and e in ATTEND_AT:
                        attend(n, c, ATTEND_AT[e][0])
                    if c is not None and e + 1 < E:
                        up(c, e + 1)
                    if n is not None and e in ATTEND_AT:
                        attend(n, c, ATTEND_AT[e][1])
                    if e == 6 and n is not None:
                        gate(n)
                    if c is not None and e in (1, DOWN_FIRST):
                        down(c, e)
                    if e == 1 and m is not None:
                        x_t(m, n)
                    if e == 1 and n is not None:
                        attend(n, c, CB)
                    if e == 2 and m is not None:
                        keys(m, n, c)
                    if e == 2 and n is not None:
                        o_t(n)
                    if e == 2 and m is not None:
                        queries(m, n)
                    if e == 3 and n is not None:
                        attn_out(n)
                    if e == 3 and m is not None:
                        values(m)
                    if e == 5 and n is not None:
                        x2_t(n, m)
                    if m is not None:
                        for b in SCORES_AT.get(e, []):
                            scores(m, b)
                    if c is not None and e not in (1, DOWN_FIRST):
                        down(c, e)

            pe.wait_ge(s_ready, 1)
            keys(0, None, None)
            x_t(0, None)
            queries(0, None)
            values(0)
            for b in range(CB):
                scores(0, b)
            pe.wait_ge(s_ready, 2)
            step(None, 0, 1)
            pe.wait_ge(s_ready, 3)
            pe.wait_ge(s_wlow, len(split_weights))
            step(0, 1, 2)
            with pe.Fori(1, NC - 2) as c:
                step(c, c + 1, c + 2)
            step(NC - 2, NC - 1, None)
            step(NC - 1, None, None)
            shared_down(NC - 1, None)
            experts_sum(NC - 1)


def kernel(x, ctx_1024, mask_BxSxS2_bk1, g_xattn, g_ffn, L0_xattn_wq, L0_xattn_bq, L0_xattn_wk, L0_xattn_bk,
           L0_xattn_wv, L0_xattn_bv, L0_xattn_wo, L0_xattn_bo, L0_ffn_gate_w, L0_ffn_w1, L0_ffn_b1, L0_ffn_w2,
           L0_ffn_b2, L0_ffn_w3, L0_ffn_b3, L0_ffn_sw1, L0_ffn_sw2, L0_ffn_sw3):
    import numpy as np
    import concourse.bacc as bacc
    from concourse.bass_utils import run_bass_kernel_spmd as run

    def t(a, *perm):
        return np.ascontiguousarray(np.transpose(np.asarray(a), perm))

    p = np.arange(P)
    consts = np.zeros((P, C_END), np.float32)
    consts[:, C_IDENT:C_IDENT + P] = np.eye(P)
    consts[:, C_IDUP:C_IDUP + S] = p[:, None] % S == np.arange(S)
    consts[:, C_HEADM:C_HEADM + G] = (p[:, None] // DH % G == np.arange(G)) * float(DH) ** -0.5
    consts[:, C_OWN:C_OWN + J] = p[:, None] // S == np.arange(J)
    consts[:, C_IOTA:C_IOTA + E] = np.arange(E)
    consts[:S, C_IDUPQ:C_IDUPQ + P] = p[:S, None] == p % S
    r = np.arange(ROWS)
    sel = (r[:, None] % E == np.arange(E)) & (r[:, None] < 3 * E)
    consts[:ROWS, C_SELW:C_SELW + E * P] = np.repeat(sel, P, axis=1)
    consts[:ROWS, C_PART:C_PART + 3] = r[:, None] // E - 3 == np.arange(3)
    consts[:ROWS, C_ROWE:C_ROWE + E] = (r[:, None] % E == np.arange(E)) & (r[:, None] >= 3 * E)

    arrays = {
        "x": t(np.reshape(x, (NC, CT, P, D)), 0, 2, 1, 3).reshape(NC, P, CT * D),
        "ctxT": t(np.reshape(ctx_1024, (NC, CHUNK, D)), 0, 2, 1),
        "mask": t(np.reshape(mask_BxSxS2_bk1, (NC, CB, S, S)), 0, 2, 1, 3).reshape(NC, S, CB * S),
        "g_x": np.reshape(g_xattn, (1,)), "g_f": np.reshape(g_ffn, (1,)),
        "wqT": t(L0_xattn_wq, 1, 0), "wkT": t(L0_xattn_wk, 1, 0),
        "wvT": t(np.reshape(t(L0_xattn_wv, 1, 0), (D, G, PR, J * DH)), 0, 2, 1, 3).reshape(D, PR, D // 2),
        "woT": t(L0_xattn_wo, 1, 0),
        "bq": np.reshape(L0_xattn_bq, (D, 1)), "bk": np.reshape(L0_xattn_bk, (D, 1)),
        "bv": np.reshape(L0_xattn_bv, (D, 1)), "bo": np.reshape(L0_xattn_bo, (D,)),
        "gateT": t(L0_ffn_gate_w, 1, 0),
        "w1T": t(L0_ffn_w1, 2, 0, 1), "w2T": t(L0_ffn_w2, 2, 0, 1), "w3T": t(L0_ffn_w3, 2, 0, 1),
        "b1T": t(L0_ffn_b1, 1, 0), "b2T": t(L0_ffn_b2, 1, 0), "b3": L0_ffn_b3,
        "sw1T": t(L0_ffn_sw1, 1, 0).reshape(D, SHARED, P), "sw2T": t(L0_ffn_sw2, 1, 0).reshape(D, SHARED, P),
        "sw3T": t(np.reshape(t(L0_ffn_sw3, 1, 0), (SHARED, P, D)), 1, 0, 2),
        "consts": consts,
    }
    nc = bacc.Bacc("TRN2", target_bir_lowering=False, num_devices=1)
    feeds, args = {}, []
    for name, a in arrays.items():
        a = np.ascontiguousarray(a)
        feeds["in_" + name] = a
        args.append(nc.dram_tensor("in_" + name, a.shape, mybir.dt.from_np(a.dtype), kind="ExternalInput").ap())
    args.append(nc.dram_tensor("out_0", (NC, P, CT * D), F32, kind="ExternalOutput").ap())
    build(nc, *args)
    got = run(nc, [feeds], core_ids=[0]).results[0]["out_0"]
    return np.ascontiguousarray(np.transpose(np.reshape(got, (NC, P, CT, D)), (0, 2, 1, 3))).reshape(B, S, D)
```

```python
from contextlib import ExitStack

import concourse.bass as bass
from concourse import mybir

F32 = mybir.dt.float32
F32R = mybir.dt.float32r
BF16 = mybir.dt.bfloat16
U8 = mybir.dt.uint8
U32 = mybir.dt.uint32
ACT = mybir.ActivationFunctionType
ALU = mybir.AluOpType
AX = mybir.AxisListType

B, S, D = 128, 64, 128
HEADS, DH = 16, 8
E = 8
P = 128
CHUNK = 512
NC = B * S // CHUNK
CB = CHUNK // S
CT = CHUNK // P
G, PR, J = 4, 2, 2
VW = DH + 1
SHARED = 2
XS = 3
NEXP = CB // 2
ROWS = 6 * E
EPS = 1e-5
MASKED = -1e20

C_IDENT = 0
C_HEADM = C_IDENT + P
C_OWN = C_HEADM + G
C_IOTA = C_OWN + J
C_IDUPQ = C_IOTA + E
C_SELW = C_IDUPQ + P
C_PART = C_SELW + E * P
C_ROWE = C_PART + 3
C_END = C_ROWE + E

SC0 = 0
SC1 = 1
PTB = 2
PVB = 3
WBB = 4
G1B = 5
G3B = 6
X2B = 7

ATTEND_AT = {0: [4, 5], 1: [6, 7]}
SCORES_AT = {3: [0, 1], 4: [2, 3], 5: [4, 5], 6: [6], 7: [7]}


def at(chunk, per_chunk, k):
    return chunk * per_chunk + k


def later(chunk):
    return not (isinstance(chunk, int) and chunk == 0)


def build(nc, x, ctxT, mask, g_x, g_f, wqT, wkT, wvT, woT, bq, bk, bv, bo, gateT, w1T, w2T, w3T,
          b1T, b2T, b3, sw1T, sw2T, sw3T, consts, out):
    with ExitStack() as ctx:
        def sb(name, shape, dt=F32):
            return ctx.enter_context(nc.sbuf_tensor(name, shape, dt))

        def sem(name):
            return ctx.enter_context(nc.semaphore(name))

        cst = sb("cst", [P, C_END])
        ident = cst[:, C_IDENT:C_IDENT + P]
        headm = cst[:, C_HEADM:C_HEADM + G]
        own = cst[:, C_OWN:C_OWN + J]
        iota = cst[:, C_IOTA:C_IOTA + E]
        ident_bf = sb("ident_bf", [P, P], BF16)
        idupq_bf = sb("idupq_bf", [S, P], BF16)
        selw = sb("selw", [P, E, P], BF16)
        b3sel = sb("b3sel", [P, E, P], BF16)
        b3row = sb("b3row", [ROWS, P])
        b3part = sb("b3part", [ROWS, 3, P], BF16)
        b3rest = sb("b3rest", [ROWS, P])
        b3pick = sb("b3pick", [ROWS, 2, P])
        wq_s, wk_s = sb("wq_s", [P, D]), sb("wk_s", [P, D])
        wv_s, wo_s = sb("wv_s", [P, PR, D // 2]), sb("wo_s", [P, D])
        gate_s = sb("gate_s", [P, E])
        w1_h, w1_l, w2_h, w2_l, w3_h, w3_l = (
            sb(n, [P, E, P], F32R) for n in ("w1_h", "w1_l", "w2_h", "w2_l", "w3_h", "w3_l"))
        sw1_h, sw1_l, sw2_h, sw2_l, sw3_h, sw3_l = (
            sb(n, [P, SHARED, P], F32R) for n in ("sw1_h", "sw1_l", "sw2_h", "sw2_l", "sw3_h", "sw3_l"))
        b1_s, b2_s = sb("b1_s", [P, E]), sb("b2_s", [P, E])
        bq_s, bk_s, bv_s = (sb(n, [P, 1]) for n in ("bq_s", "bk_s", "bv_s"))
        bqm = sb("bqm", [P, G])
        bo_s = sb("bo_s", [P, D])
        gx_s, gf_s = sb("gx_s", [P, 1]), sb("gf_s", [P, 1])
        tgx, tgf = sb("tgx", [P, 1]), sb("tgf", [P, 1])
        pow_s, eps_s = sb("pow_s", [P, CT]), sb("eps_s", [P, CT])

        xin = sb("xin", [P, CT, D])
        cT = sb("cT", [P, CHUNK])
        mk8 = sb("mk8", [S, CB, S], U8)
        mkneg = sb("mkneg", [S, CB, S], BF16)
        bn1, bn2 = sb("bn1", [P, CT, 6]), sb("bn2", [P, CT, 6])
        mv1, mv2 = sb("mv1", [P, CT, 2]), sb("mv2", [P, CT, 2])
        ve1, ve2 = sb("ve1", [P, CT]), sb("ve2", [P, CT])
        rs1, rs2 = sb("rs1", [P, CT]), sb("rs2", [P, CT])
        xn1, xn2 = sb("xn1", [P, CT, D]), sb("xn2", [P, CT, D])
        resid = sb("resid", [P, CT, D])
        xT = sb("xT", [P, CHUNK])
        qexp = sb("qexp", [P, CB, G, S])
        kexp = sb("kexp", [P, G, CHUNK])
        vexp = sb("vexp", [P, CB, G, PR * J * VW])
        smax = sb("smax", [P, 2, PR * G])
        pr = sb("pr", [P, CB, G, PR * S])
        prT = sb("prT", [P, CB, G, P])
        rden = sb("rden", [P, NEXP, 2, HEADS])
        rown = sb("rown", [P, NEXP, 2, HEADS])
        on = sb("on", [P, CB, D])
        oT0, oT = sb("oT0", [P, CHUNK]), sb("oT", [P, CHUNK])
        x1, x1k = sb("x1", [P, CT, D]), sb("x1k", [P, CT, D])
        x2T = sb("x2T", [P, CHUNK])
        lmax, lsum, lrec = sb("lmax", [P, CT]), sb("lsum", [P, CT]), sb("lrec", [P, CT])
        lsub, lexp, score = (sb(n, [P, CT, E]) for n in ("lsub", "lexp", "score"))
        top8 = sb("top8", [P, CT, 8])
        topi = sb("topi", [P, CT, 8], U32)
        is0, is1 = sb("is0", [P, CT, E]), sb("is1", [P, CT, E])
        wsel, wrest = sb("wsel", [P, CT, E]), sb("wrest", [P, CT, E])
        wm = sb("wm", [P, CT, P], BF16)
        wmT = sb("wmT", [P, CHUNK], BF16)
        sa = sb("sa", [P, SHARED, CHUNK])
        sh = sb("sh", [P, SHARED, CHUNK])
        shh, shl = sb("shh", [P, SHARED, CHUNK], F32R), sb("shl", [P, SHARED, CHUNK], F32R)
        xs = sb("xs", [P, XS, CHUNK])
        x2h, x2l = sb("x2h", [P, CHUNK], F32R), sb("x2l", [P, CHUNK], F32R)
        xh, xl = sb("xh", [P, 2, CHUNK], F32R), sb("xl", [P, 2, CHUNK], F32R)
        hb = sb("hb", [P, 2, CHUNK])
        hh, hl = sb("hh", [P, 2, CHUNK], F32R), sb("hl", [P, 2, CHUNK], F32R)
        x3 = sb("x3", [P, 2, CHUNK])
        prod = sb("prod", [P, 4, CHUNK])
        yacc, yT = sb("yacc", [P, CHUNK]), sb("yT", [P, CHUNK])
        ob = sb("ob", [P, CT, D])

        w1_s, w2_s, w3_s = (w[:, :, :].rearrange("p a (b n) -> p (a b) n", n=P) for w in (sa, hb, x3))
        sw1_s, sw2_s, sw3_s = (prod[:, k, 0:SHARED * P].rearrange("p (a n) -> p a n", n=P) for k in range(3))

        ps = ctx.enter_context(nc.psum_tensor("ps", [P, 8, 512], F32))

        s_front, s_back = sem("front_weights_loaded"), sem("back_weights_loaded")
        s_route, s_ffn = sem("route_constants_loaded"), sem("ffn_weights_loaded")
        s_set = sem("setup_step")
        s_ready = sem("setup_ready")
        s_pset = sem("pool_setup")
        s_tanh = sem("tanh_ready")
        s_x, s_ctx, s_mk, s_st = sem("x_loaded"), sem("ctx_loaded"), sem("mask_loaded"), sem("out_stored")
        s_stat1, s_stat2 = sem("ln1_moments"), sem("ln2_moments")
        s_rs2 = sem("ln2_rstd")
        s_pstep, v_step = sem("pool_own_step"), sem("dve_own_step")
        s_rs1, s_xn1, s_res, s_xn2, s_kept, s_add, s_x2l, s_xl, s_hl, s_shl, s_wlow = (sem(n) for n in (
            "ln1_rstd", "xn1_ready", "resid_ready", "xn2_ready", "x1_kept", "expert_added",
            "x2_low_part", "xs_low_part", "h_low_part", "shared_low_part", "weights_low_part"))
        p_pt, p_pv, p_ot, p_ao, p_xt, p_q, p_k, p_v = (sem(n) for n in (
            "pe_probsT", "pe_pv", "pe_oT", "pe_attn_out", "pe_xT", "pe_q", "pe_k", "pe_v"))
        p_x2t, p_gate, p_s, p_sa, p_sb, p_wmt = (sem(n) for n in (
            "pe_x2T", "pe_gate", "pe_scores", "pe_shared1", "pe_shared2", "pe_routeT"))
        p_wb, p_g1, p_g3, p_x2, p_y, p_z = (sem(n) for n in (
            "pe_weight_rows", "pe_w1", "pe_w3", "pe_w2", "pe_y", "pe_shared3"))
        a_exp, a_pt, a_ot, a_xt, a_q, a_v, a_x2t, a_ge = (sem(n) for n in (
            "act_probs", "act_probsT", "act_oT", "act_xT", "act_q", "act_v", "act_x2T", "act_gate_exp"))
        a_sa, a_h, a_x3, a_xh, a_shh, a_whigh, a_mneg = (sem(n) for n in (
            "act_shared", "act_h", "act_x3", "xs_high_part", "shared_high_part", "weights_high_part", "act_mask"))
        v_pt, v_k, v_max, v_sub, v_rec, v_norm, v_x1 = (sem(n) for n in (
            "dve_probsT", "dve_k", "dve_max", "dve_scores_shifted", "dve_sum_recip",
            "dve_o_normed", "dve_x1"))
        v_lmax, v_lsub, v_wm, v_wmt, v_sh, v_xs, v_prod, v_out, v_ot, v_yt = (sem(n) for n in (
            "dve_logit_max", "dve_logits_shifted", "dve_routes", "dve_routeT",
            "dve_shared", "dve_xs", "dve_prod", "dve_out", "dve_oT", "dve_yT"))

        def bc(ap, axis, n):
            ap = ap.unsqueeze(axis)
            shape = list(ap.shape)
            shape[axis] = n
            return ap.broadcast_to(shape)

        block = ctx.enter_context(nc.Block())

        front_loads = [
            (cst[:, 0:C_SELW], consts[:, 0:C_SELW]), (wk_s[:, :], wkT), (bk_s[:, :], bk), (bq_s[:, :], bq),
            (wq_s[:, :], wqT), (wv_s[:, :, :], wvT)]
        back_loads = [
            (gx_s[:, :], g_x.partition_broadcast(P)), (gf_s[:, :], g_f.partition_broadcast(P)),
            (bo_s[:, :], bo.partition_broadcast(P)), (wo_s[:, :], woT), (bv_s[:, :], bv), (gate_s[:, :], gateT)]
        route_loads = [(cst[:, C_SELW:C_END], consts[:, C_SELW:C_END])]
        route_loads += [(b3row[E * r:E * r + E, :], b3) for r in range(ROWS // E)]
        ffn_loads = [(b1_s[:, :], b1T), (b2_s[:, :], b2T), (sw1_s[:, :, :], sw1T), (sw2_s[:, :, :], sw2T),
                      (w1_s[:, :, :], w1T), (w3_s[:, :, :], w3T), (w2_s[:, :, :], w2T), (sw3_s[:, :, :], sw3T)]
        split_weights = [(sw1_s, sw1_h, sw1_l), (sw2_s, sw2_h, sw2_l), (w1_s, w1_h, w1_l), (w3_s, w3_h, w3_l),
                         (w2_s, w2_h, w2_l), (sw3_s, sw3_h, sw3_l)]
        ROUTE_LOADED = 16 * len(route_loads)
        FRONT_LOADED, BACK_LOADED, FFN_LOADED = 16 * len(front_loads), 16 * len(back_loads), 16 * len(ffn_loads)

        @block.sync
        def _(sp):
            def load_x(t):
                if later(t):
                    sp.wait_ge(s_xn1, t)
                    sp.wait_ge(s_res, t)
                sp.dma_start(xin[:, :, :], x[t].rearrange("p (t d) -> p t d", t=CT)).then_inc(s_x, 16)

            def load_ctx(t):
                if later(t):
                    sp.wait_ge(p_v, t)
                    sp.wait_ge(a_mneg, t)
                sp.dma_start(cT[:, :], ctxT[t]).then_inc(s_ctx, 16)
                sp.dma_start(mk8[:, :, :], mask[t].rearrange("q (b k) -> q b k", b=CB)).then_inc(s_mk, 16)

            def store(c):
                sp.wait_ge(v_out, at(c, 1, 1))
                sp.dma_start(out[c].rearrange("p (t d) -> p t d", t=CT), ob[:, :, :]).then_inc(s_st, 16)

            load_x(0)
            load_ctx(0)
            for dst, src in route_loads:
                sp.dma_start(dst, src).then_inc(s_route, 16)
            for dst, src in back_loads:
                sp.dma_start(dst, src).then_inc(s_back, 16)
            for dst, src in ffn_loads:
                sp.dma_start(dst, src).then_inc(s_ffn, 16)
            for m in (1, 2, 3):
                load_ctx(m)
                load_x(m)
            with sp.Fori(0, NC - 4) as c:
                m = sp.snap(c + 4)
                store(c)
                load_ctx(m)
                load_x(m)
            for c in range(NC - 4, NC):
                store(c)
            sp.wait_ge(s_st, 16 * NC)

        @block.gpsimd
        def _(pool):
            pool.memset(pow_s[:, :], -0.5).then_inc(s_pset, 1)
            pool.memset(eps_s[:, :], EPS).then_inc(s_pset, 1)
            pool.wait_ge(s_pset, 2)

            def rstd(stat, k, ve, rs, mv):
                pool.wait_ge(stat, at(k, 1, 1))
                pool.tensor_tensor(ve[:, :], mv[:, :, 1], eps_s[:, :], ALU.add).then_inc(s_pstep, 1)
                pool.wait_ge(s_pstep, 1)
                return pool.tensor_tensor(rs[:, :], ve[:, :], pow_s[:, :], ALU.pow)

            def front(m):
                pool.sem_clear(s_pstep)
                if later(m):
                    pool.wait_ge(s_xn1, m)
                rstd(s_stat1, m, ve1, rs1, mv1).then_inc(s_rs1, 1)

            def keep(m):
                if later(m):
                    pool.wait_ge(v_x1, m)
                pool.tensor_tensor(resid[:, :, :], xin[:, :, :], bc(bo_s[:, :], 1, CT), ALU.add).then_inc(s_res, 1)

            def back(n):
                pool.sem_clear(s_pstep)
                if later(n):
                    pool.wait_ge(s_xn2, n)
                rstd(s_stat2, n, ve2, rs2, mv2).then_inc(s_rs2, 1)

            def x2_low(n):
                pool.wait_ge(a_x2t, at(n, 1, 1))
                pool.tensor_tensor(x2l[:, :], x2T[:, :], x2h[:, :].bitcast(F32), ALU.subtract).then_inc(s_x2l, 1)

            def x_low(c, e):
                pool.wait_ge(a_xh, at(c, E, e + 1))
                pool.tensor_tensor(xl[:, e % 2, :], xs[:, e % XS, :], xh[:, e % 2, :].bitcast(F32),
                                   ALU.subtract).then_inc(s_xl, 1)

            def h_low(c, e):
                pool.wait_ge(a_h, at(c, E, e + 1))
                pool.tensor_tensor(hl[:, e % 2, :], hb[:, e % 2, :], hh[:, e % 2, :].bitcast(F32),
                                   ALU.subtract).then_inc(s_hl, 1)

            def shared_low(c, k):
                pool.wait_ge(a_shh, at(c, SHARED, k + 1))
                pool.tensor_tensor(shl[:, k, :], sh[:, k, :], shh[:, k, :].bitcast(F32), ALU.subtract).then_inc(s_shl, 1)

            def add_expert(c, e):
                pool.wait_ge(v_prod, at(c, E, e + 1))
                if e == 1:
                    if later(c):
                        pool.wait_ge(v_yt, c)
                    first = prod[:, 0, :]
                else:
                    pool.wait_ge(s_add, at(c, E - 1, e - 1))
                    first = yacc[:, :]
                pool.tensor_tensor(yacc[:, :], first, prod[:, e % 4, :], ALU.add).then_inc(s_add, 1)

            def split_low():
                for k, (whole, high, low) in enumerate(split_weights):
                    pool.wait_ge(a_whigh, k + 1)
                    pool.tensor_tensor(low[:, :, :], whole[:, :, :], high[:, :, :].bitcast(F32),
                                       ALU.subtract).then_inc(s_wlow, 1)

            def step(c, n, m):
                if c is not None:
                    x_low(c, 0)
                    x_low(c, 1)
                    if m is not None:
                        h_low(c, 0)
                for e in range(E):
                    if c is not None and e + 2 < E:
                        x_low(c, e + 2)
                    if c is not None and m is not None and e + 1 < E:
                        h_low(c, e + 1)
                    if e == 6 and n is not None:
                        x2_low(n)
                    if c is not None and e in (1, 2):
                        shared_low(c, e - 1)
                    if e == 0 and m is not None:
                        front(m)
                    if e == 0 and c is None:
                        split_low()
                    if e == 3 and n is not None:
                        back(n)
                    if c is not None and e >= 2:
                        add_expert(c, e - 1)
                    if e == 6 and m is not None:
                        keep(m)
                if c is not None:
                    add_expert(c, E - 1)

            front(0)
            pool.memset(kexp[:, :, :], 0.0).then_inc(s_pset, 1)
            pool.memset(vexp[:, :, :, :], 0.0).then_inc(s_pset, 1)
            pool.memset(wm[:, :, :], 0.0).then_inc(s_pset, 1)
            pool.memset(b3sel[:, :, :], 0.0).then_inc(s_pset, 1)
            pool.wait_ge(s_pset, 6)
            for pair in range(PR):
                ones = vexp[S * pair:S * pair + S, :, :, :].rearrange("q b g (p j n) -> q (b g) p j n", p=PR, j=J)
                pool.memset(ones[:, :, pair, :, DH], 1.0).then_inc(s_pset, 1)
            pool.wait_ge(s_ready, 3)
            keep(0)
            step(None, 0, 1)
            step(0, 1, 2)
            with pool.Fori(1, NC - 2) as c:
                step(c, c + 1, c + 2)
            step(NC - 2, NC - 1, None)
            step(NC - 1, None, None)

        @block.scalar
        def _(act):
            for dst, src in front_loads:
                act.dma_start(dst, src).then_inc(s_front, 16)

            def probs(m, i):
                act.wait_ge(v_sub, at(m, CB, 2 * i + 2))
                p2 = pr[:, 2 * i:2 * i + 2, :, :].rearrange("q b g k -> q (b g k)")
                act.activation(p2, p2, ACT.Exp).then_inc(a_exp, 1)

            def probs_t(n, b):
                act.wait_ge(p_pt, at(n, CB, b + 1))
                if later(n):
                    act.wait_ge(p_pv, at(n, NEXP, 0))
                act.activation(prT[:, b, :, :].rearrange("p g q -> p (g q)"), ps[:, PTB, :], ACT.Copy).then_inc(a_pt, 1)

            def o_t(n):
                act.wait_ge(p_ot, at(n, 1, 1))
                if later(n):
                    act.wait_ge(v_ot, n)
                for i, bank in enumerate((PVB, SC1)):
                    half = slice(CB // 2 * i, CB // 2 * (i + 1))
                    o = ps[:, bank, :].rearrange("f (b j q) -> f b j q", j=J, q=S)
                    last = act.activation(oT0[:, :].rearrange("f (b q) -> f b q", q=S)[:, half, :], o[:, :, 0, :],
                                          ACT.Identity, bias=bv_s[:, :])
                last.then_inc(a_ot, 1)

            def x_t(m):
                act.wait_ge(p_xt, at(m, 1, 1))
                if later(m):
                    act.wait_ge(p_q, m)
                act.activation(xT[:, :], ps[:, PTB, :], ACT.Copy).then_inc(a_xt, 1)

            def queries(m):
                act.wait_ge(p_q, at(m, 1, 1))
                if later(m):
                    act.wait_ge(p_s, at(m, CB, 0))
                for k in range(G):
                    last = act.activation(qexp[:, :, k, :], ps[:, PTB, :].rearrange("p (b q) -> p b q", q=S),
                                          ACT.Identity, bias=bqm[:, k:k + 1], scale=headm[:, k:k + 1])
                last.then_inc(a_q, 1)

            def values(m):
                act.wait_ge(p_v, at(m, 1, 1))
                if later(m):
                    act.wait_ge(p_pv, at(m, NEXP, 0))
                for pair in range(PR):
                    q = slice(S * pair, S * pair + S)
                    dst = vexp[q, :, :, :].rearrange("q b g (p j n) -> q (b g) p j n", p=PR, j=J)
                    last = act.activation(dst[:, :, pair, :, 0:DH],
                                          ps[q, PTB, :].rearrange("q (a j n) -> q a j n", j=J, n=DH), ACT.Copy)
                last.then_inc(a_v, 1)

            def x2_t(n):
                act.wait_ge(p_x2t, at(n, 1, 1))
                if later(n):
                    act.wait_ge(p_gate, n)
                    act.wait_ge(p_sb, at(n, SHARED, 0))
                    act.wait_ge(v_xs, at(n, E, 0))
                act.activation(x2T[:, :], ps[:, PTB, :], ACT.Copy)
                act.activation(x2h[:, :], ps[:, PTB, :], ACT.Copy).then_inc(a_x2t, 1)

            def gate_exp(n):
                act.wait_ge(v_lsub, at(n, 1, 1))
                act.activation(lexp[:, :, :], lsub[:, :, :], ACT.Exp).then_inc(a_ge, 1)

            def mask_bias(m):
                act.wait_ge(s_mk, at(m, 16, 16))
                if later(m):
                    act.wait_ge(p_s, at(m, CB, 0))
                act.activation(mkneg[:, :, :], mk8[:, :, :], ACT.Copy, scale=MASKED).then_inc(a_mneg, 1)

            def keep_x1(c):
                act.wait_ge(v_x1, at(c, 1, 1))
                if later(c):
                    act.wait_ge(v_out, c)
                act.activation(x1k[:, :, :], x1[:, :, :], ACT.Copy).then_inc(s_kept, 1)

            def shared(c, k):
                act.wait_ge(p_sa, at(c, SHARED, k + 1))
                if later(c):
                    act.wait_ge(v_sh, at(c, SHARED, 0))
                act.activation(sa[:, k, :], ps[:, G1B, :], ACT.Silu).then_inc(a_sa, 1)

            def shared_high(c, k):
                act.wait_ge(v_sh, at(c, SHARED, k + 1))
                if later(c):
                    act.wait_ge(p_z, c)
                act.activation(shh[:, k, :], sh[:, k, :], ACT.Copy).then_inc(a_shh, 1)

            def x_high(c, e):
                act.wait_ge(v_xs, at(c, E, e + 1))
                if e >= 2:
                    act.wait_ge(p_g3, at(c, E, e - 1))
                act.activation(xh[:, e % 2, :], xs[:, e % XS, :], ACT.Copy).then_inc(a_xh, 1)

            def expert(c, e):
                act.wait_ge(p_g1, at(c, E, e + 1))
                if e >= 2:
                    act.wait_ge(p_x2, at(c, E, e - 1))
                act.activation(hb[:, e % 2, :], ps[:, G1B, :], ACT.Silu, bias=b1_s[:, e:e + 1])
                act.activation(hh[:, e % 2, :], ps[:, G1B, :], ACT.Silu, bias=b1_s[:, e:e + 1]).then_inc(a_h, 1)
                act.wait_ge(p_g3, at(c, E, e + 1))
                if e >= 2:
                    act.wait_ge(v_prod, at(c, E, e - 1))
                act.activation(x3[:, e % 2, :], ps[:, G3B, :], ACT.Copy).then_inc(a_x3, 1)

            def split_high(k):
                act.wait_ge(s_ffn, FFN_LOADED)
                for whole, high, low in split_weights[k:k + 2]:
                    act.activation(high[:, :, :], whole[:, :, :], ACT.Copy).then_inc(a_whigh, 1)

            def step(c, n, m):
                if n is not None:
                    probs_t(n, 0)
                    probs(n, 2)
                    probs(n, 3)
                if c is not None:
                    shared(c, 0)
                    shared(c, 1)
                if n is not None:
                    probs_t(n, 2)
                if c is not None:
                    x_high(c, 0)
                    x_high(c, 1)
                    expert(c, 0)
                for e in range(E):
                    if c is not None and e + 2 < E:
                        x_high(c, e + 2)
                    if n is not None and e in ATTEND_AT:
                        probs_t(n, ATTEND_AT[e][0])
                    if e == 2 and n is not None:
                        o_t(n)
                    if c is not None and e + 1 < E:
                        expert(c, e + 1)
                    if e in (0, 1) and c is not None:
                        shared_high(c, e)
                    if e < 3 and c is None:
                        split_high(2 * e)
                    if e == 0 and m is not None:
                        mask_bias(m)
                    if e == 1 and m is not None:
                        x_t(m)
                    if e == 2 and m is not None:
                        queries(m)
                    if e == 1 and c is not None:
                        keep_x1(c)
                    if e == 3 and m is not None:
                        values(m)
                    if e == 5 and n is not None:
                        x2_t(n)
                if n is not None:
                    gate_exp(n)
                if m is not None:
                    probs(m, 0)
                    probs(m, 1)

            act.wait_ge(s_ready, 1)
            x_t(0)
            queries(0)
            mask_bias(0)
            act.wait_ge(s_pset, 8)
            values(0)
            act.wait_ge(s_back, BACK_LOADED)
            act.activation(tgx[:, :], gx_s[:, :], ACT.Tanh).then_inc(s_tanh, 1)
            act.activation(tgf[:, :], gf_s[:, :], ACT.Tanh).then_inc(s_tanh, 1)
            probs(0, 0)
            probs(0, 1)
            step(None, 0, 1)
            step(0, 1, 2)
            with act.Fori(1, NC - 2) as c:
                step(c, c + 1, c + 2)
            step(NC - 2, NC - 1, None)
            step(NC - 1, None, None)

        @block.vector
        def _(dve):
            setup_steps = [0]

            def setup_link(ins):
                setup_steps[0] += 1
                ins.then_inc(s_set, 1)
                dve.wait_ge(s_set, setup_steps[0])

            def setup_front():
                dve.wait_ge(s_front, FRONT_LOADED)
                dve.tensor_scalar(bqm[:, :], headm, bq_s[:, 0:1], None, ALU.mult)
                dve.tensor_copy(idupq_bf[:, :], cst[0:S, C_IDUPQ:C_IDUPQ + P]).then_inc(s_ready, 1)

            def setup_back():
                dve.wait_ge(s_back, BACK_LOADED)
                dve.wait_ge(s_tanh, 2)
                dve.tensor_scalar(wo_s[:, :], wo_s[:, :], tgx[:, 0:1], None, ALU.mult)
                dve.tensor_scalar(bo_s[:, :], bo_s[:, :], tgx[:, 0:1], None, ALU.mult).then_inc(s_ready, 1)

            def setup_route():
                dve.wait_ge(s_route, ROUTE_LOADED)
                dve.tensor_copy(ident_bf[:, :], ident)
                dve.tensor_copy(selw[:, :, :].rearrange("r e p -> r (e p)"), cst[:, C_SELW:C_SELW + E * P])
                setup_link(dve.tensor_copy(b3part[:, 0, :], b3row[:, :]))
                setup_link(dve.tensor_tensor(b3rest[:, :], b3row[:, :], b3part[:, 0, :], ALU.subtract))
                setup_link(dve.tensor_copy(b3part[:, 1, :], b3rest[:, :]))
                setup_link(dve.tensor_tensor(b3part[:, 2, :], b3rest[:, :], b3part[:, 1, :], ALU.subtract))
                part = [cst[0:ROWS, C_PART + k:C_PART + k + 1] for k in range(3)]
                setup_link(dve.tensor_scalar(b3pick[:, 0, :], b3part[:, 0, :], part[0], None, ALU.mult))
                setup_link(dve.scalar_tensor_tensor(b3pick[:, 1, :], b3part[:, 1, :], part[1], b3pick[:, 0, :],
                                                    ALU.mult, ALU.add))
                setup_link(dve.scalar_tensor_tensor(b3pick[:, 0, :], b3part[:, 2, :], part[2], b3pick[:, 1, :],
                                                    ALU.mult, ALU.add))
                for e in range(E):
                    last = dve.tensor_scalar(b3sel[0:ROWS, e, :], b3pick[:, 0, :],
                                             cst[0:ROWS, C_ROWE + e:C_ROWE + e + 1], None, ALU.mult)
                last.then_inc(s_ready, 1)

            def stats(src, bn, mv, done):
                for i in range(CT):
                    last = dve.bn_stats(bn[:, i, :], src[:, i, :])
                last.then_inc(v_step, 1)
                dve.wait_ge(v_step, 1)
                for i in range(CT):
                    last = dve.bn_aggr(mv[:, i, :], bn[:, i, :])
                last.then_inc(done, 1)

            def front_stats(m):
                dve.sem_clear(v_step)
                dve.wait_ge(s_x, at(m, 16, 16))
                if later(m):
                    dve.wait_ge(s_rs1, m)
                stats(xin, bn1, mv1, s_stat1)

            def ln1(m):
                dve.wait_ge(s_rs1, at(m, 1, 1))
                if later(m):
                    dve.wait_ge(p_xt, m)
                for i in range(CT):
                    last = dve.tensor_scalar(xn1[:, i, :], xin[:, i, :], mv1[:, i, 0:1], rs1[:, i:i + 1],
                                             ALU.subtract, ALU.mult)
                last.then_inc(s_xn1, 1)

            def probs_t(n, b):
                dve.wait_ge(p_pt, at(n, CB, b + 1))
                if later(n):
                    dve.wait_ge(p_pv, at(n, NEXP, 0))
                dve.tensor_copy(prT[:, b, :, :].rearrange("p g q -> p (g q)"), ps[:, PTB, :]).then_inc(v_pt, 1)

            def norm(n, i):
                dve.wait_ge(p_pv, at(n, NEXP, i + 1))
                o = ps[:, SC1 if i % 2 else PVB, :].rearrange("q (s w) -> q s w", s=2)[:, :, 0:HEADS * VW].rearrange(
                    "q b (h n) -> q b h n", n=VW)
                dve.reciprocal(rden[:, i, :, :], o[:, :, :, DH]).then_inc(v_rec, 1)
                dve.wait_ge(v_rec, at(n, 2 * NEXP, 2 * i + 1))
                dve.tensor_tensor(rown[:, i, :, :].rearrange("q b (a j) -> q (b a) j", j=J),
                                  rden[:, i, :, :].rearrange("q b (a j) -> q (b a) j", j=J),
                                  bc(own, 1, 2 * HEADS // J), ALU.mult).then_inc(v_rec, 1)
                dve.wait_ge(v_rec, at(n, 2 * NEXP, 2 * i + 2))
                if later(n):
                    dve.wait_ge(p_ot, n)
                dve.tensor_tensor(on[:, 2 * i:2 * i + 2, :].rearrange("q b (h d) -> q b h d", d=DH),
                                  o[:, :, :, 0:DH], bc(rown[:, i, :, :], 3, DH), ALU.mult).then_inc(v_norm, 1)

            def o_t(n):
                dve.wait_ge(a_ot, at(n, 1, 1))
                if later(n):
                    dve.wait_ge(p_ao, n)
                for i, bank in enumerate((PVB, SC1)):
                    half = slice(CB // 2 * i, CB // 2 * (i + 1))
                    o = ps[:, bank, :].rearrange("f (b j q) -> f b j q", j=J, q=S)
                    last = dve.tensor_tensor(oT[:, :].rearrange("f (b q) -> f b q", q=S)[:, half, :], o[:, :, 1, :],
                                             oT0[:, :].rearrange("f (b q) -> f b q", q=S)[:, half, :], ALU.add)
                last.then_inc(v_ot, 1)

            def residual(n):
                dve.sem_clear(v_step)
                dve.wait_ge(p_ao, at(n, 1, 1))
                dve.wait_ge(s_res, at(n, 1, 1))
                if later(n):
                    dve.wait_ge(s_kept, n)
                dve.tensor_tensor(x1[:, :, :], ps[:, PVB, :].rearrange("q (t d) -> q t d", t=CT), resid[:, :, :],
                                  ALU.add).then_inc(v_x1, 1)
                dve.wait_ge(v_x1, at(n, 1, 1))
                stats(x1, bn2, mv2, s_stat2)

            def ln2(n):
                dve.wait_ge(s_rs2, at(n, 1, 1))
                if later(n):
                    dve.wait_ge(p_x2t, n)
                for i in range(CT):
                    last = dve.tensor_scalar(xn2[:, i, :], x1[:, i, :], mv2[:, i, 0:1], rs2[:, i:i + 1],
                                             ALU.subtract, ALU.mult)
                last.then_inc(s_xn2, 1)

            def keys(m):
                dve.wait_ge(p_k, at(m, 1, 1))
                if later(m):
                    dve.wait_ge(p_s, at(m, CB, 0))
                for g in range(G):
                    q = slice(32 * g, 32 * g + 32)
                    last = dve.tensor_scalar(kexp[q, g, :], ps[q, SC0, :], bk_s[q, 0:1], None, ALU.add)
                last.then_inc(v_k, 1)

            def gate_max(n):
                logit = ps[:, PVB, 0:CT * E].rearrange("q (t e) -> q t e", e=E)
                dve.wait_ge(p_gate, at(n, 1, 1))
                dve.reduce_max(lmax[:, :], logit, AX.X).then_inc(v_lmax, 1)
                dve.wait_ge(v_lmax, at(n, 1, 1))
                dve.tensor_tensor(lsub[:, :, :], logit, bc(lmax[:, :], 2, E), ALU.subtract).then_inc(v_lsub, 1)

            def route(c):
                n = [0]

                def link(ins):
                    n[0] += 1
                    ins.then_inc(v_step, 1)
                    dve.wait_ge(v_step, n[0])

                dve.sem_clear(v_step)
                dve.wait_ge(a_ge, at(c, 1, 1))
                link(dve.reduce_sum(lsum[:, :], lexp[:, :, :], AX.X))
                link(dve.reciprocal(lrec[:, :], lsum[:, :]))
                link(dve.tensor_tensor(score[:, :, :], lexp[:, :, :], bc(lrec[:, :], 2, E), ALU.mult))
                for i in range(CT):
                    last = dve.max(top8[:, i, :], score[:, i, :])
                link(last)
                for i in range(CT):
                    last = dve.max_index(topi[:, i, :], top8[:, i, :], score[:, i, :])
                link(last)
                dve.tensor_tensor(is0[:, :, :], bc(iota, 1, CT), bc(topi[:, :, 0], 2, E), ALU.is_equal)
                link(dve.tensor_tensor(is1[:, :, :], bc(iota, 1, CT), bc(topi[:, :, 1], 2, E), ALU.is_equal))
                if later(c):
                    dve.wait_ge(p_wmt, c)
                link(dve.tensor_tensor(is1[:, :, :], is0[:, :, :], is1[:, :, :], ALU.add))
                dve.tensor_copy(wm[:, :, 3 * E:ROWS].rearrange("q t (r e) -> q t r e", r=3), bc(is1[:, :, :], 2, 3))
                link(dve.tensor_tensor(wsel[:, :, :], score[:, :, :], is1[:, :, :], ALU.mult))
                link(dve.tensor_copy(wm[:, :, 0:E], wsel[:, :, :]))
                link(dve.tensor_tensor(wrest[:, :, :], wsel[:, :, :], wm[:, :, 0:E], ALU.subtract))
                link(dve.tensor_copy(wm[:, :, E:2 * E], wrest[:, :, :]))
                dve.tensor_tensor(wm[:, :, 2 * E:3 * E], wrest[:, :, :], wm[:, :, E:2 * E],
                                  ALU.subtract).then_inc(v_wm, 1)

            def scores(m, b):
                s4 = ps[:, SC1 if b % 2 else SC0, :].rearrange("q (a k) -> q a k", k=S)
                dve.wait_ge(p_s, at(m, CB, b + 1))
                dve.reduce_max(smax[:, b % 2, :], s4, AX.X).then_inc(v_max, 1)
                dve.wait_ge(v_max, at(m, CB, b + 1))
                if later(m):
                    dve.wait_ge(p_pt, at(m, CB, 0))
                dve.tensor_tensor(pr[:, b, :, :].rearrange("q g (p k) -> q (g p) k", k=S), s4,
                                  bc(smax[:, b % 2, :], 2, S), ALU.subtract).then_inc(v_sub, 1)

            def shared(c, k):
                dve.wait_ge(a_sa, at(c, SHARED, k + 1))
                dve.wait_ge(p_sb, at(c, SHARED, k + 1))
                if later(c):
                    dve.wait_ge(s_shl, at(c, SHARED, 0))
                dve.tensor_tensor(sh[:, k, :], ps[:, G3B, :], sa[:, k, :], ALU.mult).then_inc(v_sh, 1)

            def routes_t(c):
                dve.wait_ge(p_wmt, at(c, 1, 1))
                if later(c):
                    dve.wait_ge(p_g3, at(c, E, 0))
                dve.tensor_copy(wmT[:, :], ps[:, WBB, 0:CHUNK // 2].bitcast(BF16)).then_inc(v_wmt, 1)

            def scale_x(c, e):
                dve.wait_ge(p_wb, at(c, E, e + 1))
                if e >= XS:
                    dve.wait_ge(s_xl, at(c, E, e - XS + 1))
                dve.tensor_tensor(xs[:, e % XS, :], ps[:, WBB, :], x2T[:, :], ALU.mult).then_inc(v_xs, 1)

            def combine(c, e):
                dve.wait_ge(p_x2, at(c, E, e + 1))
                dve.wait_ge(a_x3, at(c, E, e + 1))
                if e >= 4:
                    dve.wait_ge(s_add, at(c, E - 1, max(e - 4, 1)))
                elif later(c):
                    dve.wait_ge(s_add, at(c, E - 1, 0))
                dve.scalar_tensor_tensor(prod[:, e % 4, :], ps[:, X2B, :], b2_s[:, e:e + 1], x3[:, e % 2, :],
                                         ALU.add, ALU.mult).then_inc(v_prod, 1)

            def h_low(c, e):
                dve.wait_ge(a_h, at(c, E, e + 1))
                dve.tensor_tensor(hl[:, e % 2, :], hb[:, e % 2, :], hh[:, e % 2, :].bitcast(F32),
                                  ALU.subtract).then_inc(s_hl, 1)

            def sum_up(c):
                dve.wait_ge(p_z, at(c, 1, 1))
                dve.wait_ge(s_add, at(c, E - 1, E - 1))
                if later(c):
                    dve.wait_ge(p_y, c)
                dve.tensor_tensor(yT[:, :], ps[:, SC0, :], yacc[:, :], ALU.add).then_inc(v_yt, 1)

            def output(c):
                dve.wait_ge(p_y, at(c, 1, 1))
                dve.wait_ge(s_kept, at(c, 1, 1))
                if later(c):
                    dve.wait_ge(s_st, at(c, 16, 0))
                dve.scalar_tensor_tensor(ob[:, :, :].rearrange("q t d -> q (t d)"), ps[:, SC0, :], tgf[:, 0:1],
                                         x1k[:, :, :].rearrange("q t d -> q (t d)"), ALU.mult, ALU.add).then_inc(v_out, 1)

            def step(c, n, m):
                if c is not None:
                    routes_t(c)
                if n is not None:
                    probs_t(n, 1)
                if c is not None:
                    shared(c, 0)
                    scale_x(c, 0)
                    shared(c, 1)
                    scale_x(c, 1)
                if n is not None:
                    norm(n, 0)
                    probs_t(n, 3)
                if c is not None:
                    scale_x(c, 2)
                if c is not None and m is None:
                    h_low(c, 0)
                for e in range(E):
                    if c is not None and 1 <= e < E - XS:
                        scale_x(c, e + XS)
                    if e == 0 and c is not None and later(c):
                        sum_up(c - 1)
                    if e == 0 and m is not None:
                        front_stats(m)
                    if e == 1 and c is not None and later(c):
                        output(c - 1)
                    if e == 1 and m is not None:
                        ln1(m)
                    if n is not None and e in ATTEND_AT:
                        norm(n, ATTEND_AT[e][0] // 2 - 1)
                    if c is not None and e == 0:
                        scale_x(c, XS)
                    if n is not None and e in ATTEND_AT:
                        probs_t(n, ATTEND_AT[e][1])
                    if e == 1 and n is not None:
                        norm(n, NEXP - 1)
                    if c is not None and m is None and e + 1 < E:
                        h_low(c, e + 1)
                    if e == 2 and n is not None:
                        o_t(n)
                    if e == 2 and c is not None:
                        combine(c, e)
                    if e == 2 and m is not None:
                        keys(m)
                    if e == 3 and n is not None:
                        residual(n)
                    if e == 6 and n is not None:
                        gate_max(n)
                    if c is not None and e in (3, 6):
                        combine(c, e)
                    if e == 4 and n is not None:
                        ln2(n)
                    if m is not None:
                        for b in SCORES_AT.get(e, []):
                            scores(m, b)
                    if e == 7 and n is not None:
                        route(n)
                    if c is not None and e not in (2, 3, 6):
                        combine(c, e)

            front_stats(0)
            setup_front()
            ln1(0)
            dve.wait_ge(s_pset, 8)
            keys(0)
            setup_route()
            setup_back()
            for b in range(CB):
                scores(0, b)
            step(None, 0, 1)
            step(0, 1, 2)
            with dve.Fori(1, NC - 2) as c:
                step(c, c + 1, c + 2)
            step(NC - 2, NC - 1, None)
            step(NC - 1, None, None)
            sum_up(NC - 1)
            output(NC - 1)

        @block.tensor
        def _(pe):
            def product(bank, w_high, w_low, x_high, x_low, start, stop=True):
                pe.matmul(ps[:, bank, :], w_low, x_high, start=start, stop=False)
                pe.matmul(ps[:, bank, :], w_high, x_low, start=False, stop=False)
                return pe.matmul(ps[:, bank, :], w_high, x_high, start=False, stop=stop)

            def probs_t(n, c, b):
                if b % 2 == 0:
                    pe.wait_ge(a_exp, at(n, NEXP, b // 2 + 1))
                if b == 0:
                    pe.wait_ge(a_v, at(n, 1, 1))
                    if c is not None:
                        pe.wait_ge(a_x2t, at(c, 1, 1))
                elif b % 2:
                    pe.wait_ge(a_pt, at(n, NEXP, b // 2 + 1))
                else:
                    pe.wait_ge(v_pt, at(n, NEXP, b // 2))
                for g in range(G):
                    last = pe.transpose(ps[:, PTB, g * P:g * P + P], pr[:, b, g, :], ident)
                last.then_inc(p_pt, 1)

            def pv(n, c, b):
                if b == 0 and c is not None:
                    pe.wait_ge(v_lsub, at(c, 1, 1))
                if b == 2:
                    pe.wait_ge(v_sub, at(n, CB, CB))
                if b % 2 == 0 and b >= 4:
                    pe.wait_ge(v_norm, at(n, NEXP, b // 2 - 1))
                if b % 2:
                    pe.wait_ge(v_pt, at(n, NEXP, b // 2 + 1))
                else:
                    pe.wait_ge(a_pt, at(n, NEXP, b // 2 + 1))
                bank = SC1 if b // 2 % 2 else PVB
                w = PR * J * VW
                for g in range(G):
                    last = pe.matmul(ps[:, bank, 256 * (b % 2) + w * g:256 * (b % 2) + w * g + w],
                                     prT[:, b, g, :], vexp[:, b, g, :], start=True, stop=True)
                if b % 2:
                    last.then_inc(p_pv, 1)

            def attend(n, c, b):
                if b < CB:
                    probs_t(n, c, b)
                if b:
                    pv(n, c, b - 1)

            def o_t(n):
                pe.wait_ge(v_norm, at(n, NEXP, NEXP))
                for b in range(CB):
                    i = b % (CB // 2)
                    last = pe.transpose(ps[:, SC1 if b >= CB // 2 else PVB, P * i:P * i + P], on[:, b, :], ident)
                last.then_inc(p_ot, 1)

            def attn_out(n):
                pe.wait_ge(v_ot, at(n, 1, 1))
                for i in range(CT):
                    last = pe.matmul(ps[:, PVB, P * i:P * i + P], oT[:, P * i:P * i + P], wo_s[:, :],
                                     start=True, stop=True)
                last.then_inc(p_ao, 1)

            def x_t(m, n):
                pe.wait_ge(s_xn1, at(m, 1, 1))
                if n is not None:
                    pe.wait_ge(v_pt, at(n, NEXP, NEXP))
                for i in range(CT):
                    last = pe.transpose(ps[:, PTB, P * i:P * i + P], xn1[:, i, :], ident)
                last.then_inc(p_xt, 1)

            def queries(m):
                pe.wait_ge(a_xt, at(m, 1, 1))
                pe.matmul(ps[:, PTB, :], wq_s[:, :], xT[:, :], start=True, stop=True).then_inc(p_q, 1)

            def keys(m, n, c):
                pe.wait_ge(s_ctx, at(m, 16, 16))
                if c is not None and later(c):
                    pe.wait_ge(v_out, c)
                elif n is not None:
                    pe.wait_ge(v_sub, at(n, CB, CB))
                pe.matmul(ps[:, SC0, :], wk_s[:, :], cT[:, :], start=True, stop=True).then_inc(p_k, 1)

            def values(m):
                pe.wait_ge(a_q, at(m, 1, 1))
                for b in range(CB):
                    for pair in range(PR):
                        last = pe.matmul(ps[S * pair:S * pair + S, PTB, S * b:S * b + S], cT[:, S * b:S * b + S],
                                         wv_s[:, pair, :], start=True, stop=True)
                last.then_inc(p_v, 1)

            def scores(m, n, b):
                if b == 0:
                    pe.wait_ge(a_q, at(m, 1, 1))
                    if n is not None:
                        pe.wait_ge(v_ot, at(n, 1, 1))
                    pe.wait_ge(v_k, at(m, 1, 1))
                    pe.wait_ge(a_mneg, at(m, 1, 1))
                if b >= 2:
                    pe.wait_ge(v_sub, at(m, CB, b - 1))
                bank = SC1 if b % 2 else SC0
                pe.matmul(ps[:, bank, :].rearrange("q (a k) -> q a k", k=S), idupq_bf[:, :],
                          bc(mkneg[:, b, :], 1, PR * G), start=True, stop=False)
                for pair in range(PR):
                    last = pe.matmul(ps[:, bank, :].rearrange("q (g p k) -> q g p k", g=G, p=PR)[:, :, pair, :],
                                     qexp[:, b, 2 * pair:2 * pair + 2, :].rearrange("f m q -> f (m q)"),
                                     kexp[:, :, S * b:S * b + S], start=False, stop=(pair == PR - 1))
                last.then_inc(p_s, 1)

            def x2_t(n, m):
                pe.wait_ge(s_xn2, at(n, 1, 1))
                if m is not None:
                    pe.wait_ge(a_v, at(m, 1, 1))
                else:
                    pe.wait_ge(v_pt, at(n, NEXP, NEXP))
                for i in range(CT):
                    last = pe.transpose(ps[:, PTB, P * i:P * i + P], xn2[:, i, :], ident)
                last.then_inc(p_x2t, 1)

            def gate(n):
                pe.wait_ge(a_x2t, at(n, 1, 1))
                pe.wait_ge(v_x1, at(n, 1, 1))
                for i in range(CT):
                    last = pe.matmul(ps[:, PVB, E * i:E * i + E], x2T[:, P * i:P * i + P], gate_s[:, :],
                                     start=True, stop=True)
                last.then_inc(p_gate, 1)

            def shared_first(c, k):
                if k:
                    pe.wait_ge(a_sa, at(c, SHARED, k))
                elif later(c):
                    pe.wait_ge(a_h, at(c, E, 0))
                if not k:
                    pe.wait_ge(s_x2l, at(c, 1, 1))
                product(G1B, sw1_h[:, k, :], sw1_l[:, k, :], x2h[:, :], x2l[:, :], True).then_inc(p_sa, 1)

            def shared_second(c, k):
                if k:
                    pe.wait_ge(v_sh, at(c, SHARED, k))
                elif later(c):
                    pe.wait_ge(a_x3, at(c, E, 0))
                product(G3B, sw2_h[:, k, :], sw2_l[:, k, :], x2h[:, :], x2l[:, :], True).then_inc(p_sb, 1)

            def routes_t(c):
                pe.wait_ge(v_wm, at(c, 1, 1))
                if later(c):
                    pe.wait_ge(v_xs, at(c, E, 0))
                for i in range(CT):
                    last = pe.transpose(ps[:, WBB, P // 2 * i:P // 2 * i + P // 2].bitcast(BF16), wm[:, i, :],
                                        ident_bf[:, :])
                last.then_inc(p_wmt, 1)

            def weight_rows(c, e):
                if e:
                    pe.wait_ge(v_xs, at(c, E, e))
                else:
                    pe.wait_ge(v_wmt, at(c, 1, 1))
                pe.matmul(ps[:, WBB, :], selw[:, e, :], wmT[:, :], start=True, stop=True).then_inc(p_wb, 1)

            def up(c, e):
                pe.wait_ge(s_xl, at(c, E, e + 1))
                if e:
                    pe.wait_ge(a_h, at(c, E, e))
                else:
                    pe.wait_ge(a_sa, at(c, SHARED, SHARED))
                product(G1B, w1_h[:, e, :], w1_l[:, e, :], xh[:, e % 2, :], xl[:, e % 2, :], True).then_inc(p_g1, 1)
                if e:
                    pe.wait_ge(a_x3, at(c, E, e))
                else:
                    pe.wait_ge(v_sh, at(c, SHARED, SHARED))
                pe.matmul(ps[:, G3B, :], b3sel[:, e, :], wmT[:, :], start=True, stop=False)
                product(G3B, w3_h[:, e, :], w3_l[:, e, :], xh[:, e % 2, :], xl[:, e % 2, :], False).then_inc(p_g3, 1)

            def down(c, e):
                pe.wait_ge(s_hl, at(c, E, e + 1))
                if e:
                    pe.wait_ge(v_prod, at(c, E, e))
                elif later(c):
                    pe.wait_ge(v_prod, at(c, E, 0))
                product(X2B, w2_h[:, e, :], w2_l[:, e, :], hh[:, e % 2, :], hl[:, e % 2, :], True).then_inc(p_x2, 1)

            def shared_down(c, m):
                pe.wait_ge(s_shl, at(c, SHARED, SHARED))
                if m is not None:
                    pe.wait_ge(v_sub, at(m, CB, CB - 1))
                else:
                    pe.wait_ge(v_out, c)
                product(SC0, sw3_h[:, 0, :], sw3_l[:, 0, :], shh[:, 0, :], shl[:, 0, :], True, False)
                product(SC0, sw3_h[:, 1, :], sw3_l[:, 1, :], shh[:, 1, :], shl[:, 1, :], False).then_inc(p_z, 1)

            def result_t(c):
                pe.wait_ge(v_yt, at(c, 1, 1))
                for i in range(CT):
                    last = pe.transpose(ps[:, SC0, P * i:P * i + P], yT[:, P * i:P * i + P], ident)
                last.then_inc(p_y, 1)

            def step(c, n, m):
                if n is not None:
                    attend(n, c, 0)
                if c is not None:
                    shared_first(c, 0)
                    shared_second(c, 0)
                    if later(c):
                        shared_down(c - 1, n)
                if n is not None:
                    attend(n, c, 1)
                if c is not None:
                    routes_t(c)
                    shared_first(c, 1)
                    weight_rows(c, 0)
                if n is not None:
                    attend(n, c, 2)
                if c is not None:
                    shared_second(c, 1)
                    weight_rows(c, 1)
                if n is not None:
                    attend(n, c, 3)
                if c is not None:
                    up(c, 0)
                    weight_rows(c, 2)
                for e in range(E):
                    if c is not None and 1 <= e < E - XS:
                        weight_rows(c, e + XS)
                    if n is not None and e in ATTEND_AT:
                        attend(n, c, ATTEND_AT[e][0])
                    if c is not None and e == 0:
                        weight_rows(c, XS)
                    if c is not None and e + 1 < E:
                        up(c, e + 1)
                    if e == 2 and n is not None:
                        o_t(n)
                    if e == 3 and n is not None:
                        attn_out(n)
                    if e == 6 and n is not None:
                        gate(n)
                    if n is not None and e in ATTEND_AT:
                        attend(n, c, ATTEND_AT[e][1])
                    if e == 0 and c is not None and later(c):
                        result_t(c - 1)
                    if c is not None and e in (1, 2, 3, 6):
                        down(c, e)
                    if e == 2 and m is not None:
                        keys(m, n, c)
                        queries(m)
                    if e == 1 and m is not None:
                        x_t(m, n)
                    if e == 1 and n is not None:
                        attend(n, c, CB)
                    if e == 3 and m is not None:
                        values(m)
                    if e == 5 and n is not None:
                        x2_t(n, m)
                    if m is not None:
                        for b in SCORES_AT.get(e, []):
                            scores(m, n, b)
                    if c is not None and e not in (1, 2, 3, 6):
                        down(c, e)

            pe.wait_ge(s_ready, 1)
            keys(0, None, None)
            x_t(0, None)
            queries(0)
            values(0)
            for b in range(CB):
                scores(0, None, b)
            pe.wait_ge(s_ready, 3)
            step(None, 0, 1)
            pe.wait_ge(s_wlow, len(split_weights))
            step(0, 1, 2)
            with pe.Fori(1, NC - 2) as c:
                step(c, c + 1, c + 2)
            step(NC - 2, NC - 1, None)
            step(NC - 1, None, None)
            shared_down(NC - 1, None)
            result_t(NC - 1)


def kernel(x, ctx_1024, mask_BxSxS2_bk1, g_xattn, g_ffn, L0_xattn_wq, L0_xattn_bq, L0_xattn_wk, L0_xattn_bk,
           L0_xattn_wv, L0_xattn_bv, L0_xattn_wo, L0_xattn_bo, L0_ffn_gate_w, L0_ffn_w1, L0_ffn_b1, L0_ffn_w2,
           L0_ffn_b2, L0_ffn_w3, L0_ffn_b3, L0_ffn_sw1, L0_ffn_sw2, L0_ffn_sw3):
    import numpy as np
    import concourse.bacc as bacc
    from concourse.bass_utils import run_bass_kernel_spmd as run

    def t(a, *perm):
        return np.ascontiguousarray(np.transpose(np.asarray(a), perm))

    p = np.arange(P)
    consts = np.zeros((P, C_END), np.float32)
    consts[:, C_IDENT:C_IDENT + P] = np.eye(P)
    consts[:, C_HEADM:C_HEADM + G] = (p[:, None] // DH % G == np.arange(G)) * float(DH) ** -0.5
    consts[:, C_OWN:C_OWN + J] = p[:, None] // S == np.arange(J)
    consts[:, C_IOTA:C_IOTA + E] = np.arange(E)
    consts[:S, C_IDUPQ:C_IDUPQ + P] = p[:S, None] == p % S
    r = np.arange(ROWS)
    sel = (r[:, None] % E == np.arange(E)) & (r[:, None] < 3 * E)
    consts[:ROWS, C_SELW:C_SELW + E * P] = np.repeat(sel, P, axis=1)
    consts[:ROWS, C_PART:C_PART + 3] = r[:, None] // E - 3 == np.arange(3)
    consts[:ROWS, C_ROWE:C_ROWE + E] = (r[:, None] % E == np.arange(E)) & (r[:, None] >= 3 * E)

    arrays = {
        "x": t(np.reshape(x, (NC, CT, P, D)), 0, 2, 1, 3).reshape(NC, P, CT * D),
        "ctxT": t(np.reshape(ctx_1024, (NC, CHUNK, D)), 0, 2, 1),
        "mask": t(np.reshape(mask_BxSxS2_bk1, (NC, CB, S, S)), 0, 2, 1, 3).reshape(NC, S, CB * S),
        "g_x": np.reshape(g_xattn, (1,)), "g_f": np.reshape(g_ffn, (1,)),
        "wqT": t(L0_xattn_wq, 1, 0), "wkT": t(L0_xattn_wk, 1, 0),
        "wvT": t(np.reshape(t(L0_xattn_wv, 1, 0), (D, G, PR, J * DH)), 0, 2, 1, 3).reshape(D, PR, D // 2),
        "woT": t(L0_xattn_wo, 1, 0),
        "bq": np.reshape(L0_xattn_bq, (D, 1)), "bk": np.reshape(L0_xattn_bk, (D, 1)),
        "bv": np.reshape(L0_xattn_bv, (D, 1)), "bo": np.reshape(L0_xattn_bo, (D,)),
        "gateT": t(L0_ffn_gate_w, 1, 0),
        "w1T": t(L0_ffn_w1, 2, 0, 1), "w2T": t(L0_ffn_w2, 2, 0, 1), "w3T": t(L0_ffn_w3, 2, 0, 1),
        "b1T": t(L0_ffn_b1, 1, 0), "b2T": t(L0_ffn_b2, 1, 0), "b3": L0_ffn_b3,
        "sw1T": t(L0_ffn_sw1, 1, 0).reshape(D, SHARED, P), "sw2T": t(L0_ffn_sw2, 1, 0).reshape(D, SHARED, P),
        "sw3T": t(np.reshape(t(L0_ffn_sw3, 1, 0), (SHARED, P, D)), 1, 0, 2),
        "consts": consts,
    }
    nc = bacc.Bacc("TRN2", target_bir_lowering=False, num_devices=1)
    feeds, args = {}, []
    for name, a in arrays.items():
        a = np.ascontiguousarray(a)
        feeds["in_" + name] = a
        args.append(nc.dram_tensor("in_" + name, a.shape, mybir.dt.from_np(a.dtype), kind="ExternalInput").ap())
    args.append(nc.dram_tensor("out_0", (NC, P, CT * D), F32, kind="ExternalOutput").ap())
    build(nc, *args)
    got = run(nc, [feeds], core_ids=[0]).results[0]["out_0"]
    return np.ascontiguousarray(np.transpose(np.reshape(got, (NC, P, CT, D)), (0, 2, 1, 3))).reshape(B, S, D)
```
